# Optimizing a Trainium2 kernel written in Bass

```python
import numpy as np
import jax
import jax.numpy as jnp

def _softmax(x, axis=-1):
    return jax.nn.softmax(x, axis=axis)

def _gelu(x):
    return jax.nn.gelu(x, approximate=True)

def _silu(x):
    return jax.nn.silu(x)

def _sigmoid(x):
    return jax.nn.sigmoid(x)

def _layernorm(x, axis=-1, eps=1e-05):
    m = jnp.mean(x, axis=axis, keepdims=True)
    v = jnp.var(x, axis=axis, keepdims=True)
    return (x - m) / jnp.sqrt(v + eps)

def _scatter_add(tgt, idx, src, axis=0):
    return tgt.at[idx].add(src)

def _segment_sum(src, seg, n):
    return jax.ops.segment_sum(src, seg, n)
kernel_name = 'mk_vit_tower_cls_d1_tok_img768_r4_c4cada'

def setup_inputs(seed: int=0):
    np.random.seed(seed)
    _w = jnp.asarray

    def _rec_inputs():
        import jax
        import jax.numpy as jnp
        _rk = jax.random.key(seed)
        x = -0.000596345 + 1.00056 * jax.random.normal(jax.random.fold_in(_rk, 1), (2, 3, 64, 64), jnp.float32)
        cls_tok = 0.02 * jax.random.normal(jax.random.fold_in(_rk, 5), (1, 1, 192), jnp.float32)
        return (x, cls_tok)
    x, cls_tok = _rec_inputs()

    def _L0_tok_setup():
        import jax, jax.numpy as jnp
        import numpy as np
        B = 16
        IMG = 64
        CH = 3
        EMBED = 64
        GP = 16
        PRE = [1, 2, 4]
        N_LEVELS = 3
        FUSED = EMBED * N_LEVELS

        def hilbert_flat_indices(n):
            t = np.arange(n * n, dtype=np.int64)
            x = np.zeros(n * n, dtype=np.int64)
            y = np.zeros(n * n, dtype=np.int64)
            s = 1
            while s < n:
                rx = 1 & t // 2
                ry = 1 & (t ^ rx)
                swap = ry == 0
                flip = swap & (rx == 1)
                x = np.where(flip, s - 1 - x, x)
                y = np.where(flip, s - 1 - y, y)
                x2 = np.where(swap, y, x)
                y2 = np.where(swap, x, y)
                x, y = (x2, y2)
                x = x + s * rx
                y = y + s * ry
                t = t // 4
                s *= 2
            return y * n + x

        def _level(x, idx, W, b, p, gp):
            Bsz, C, H, _ = x.shape
            h = H // p
            t = x.reshape(Bsz, C, h, p, h, p).transpose(0, 2, 4, 3, 5, 1).reshape(Bsz, h * h, p * p * C)
            t = t[:, idx]
            t = t.reshape(Bsz, h * h // gp, gp * p * p * C)
            return t @ W.T + b

        def _interp_linear(x, n_out):
            L = x.shape[1]
            pos = (jnp.arange(n_out, dtype=jnp.float32) + 0.5) * (L / n_out) - 0.5
            pos = jnp.clip(pos, 0.0, L - 1)
            i0 = jnp.floor(pos).astype(jnp.int32)
            i1 = jnp.minimum(i0 + 1, L - 1)
            w = (pos - i0).astype(x.dtype)
            return x[:, i0] * (1.0 - w)[None, :, None] + x[:, i1] * w[None, :, None]
        key = jax.random.key(seed)
        ks = jax.random.split(key, 9)
        inp = {'x': jax.random.normal(ks[0], (B, CH, IMG, IMG), jnp.float32)}
        for i, p in enumerate(PRE):
            din = CH * p * p * GP
            inp[f'W{i}'] = jax.random.normal(ks[1 + 2 * i], (EMBED, din), jnp.float32) * din ** (-0.5)
            inp[f'b{i}'] = jax.random.normal(ks[2 + 2 * i], (EMBED,), jnp.float32) * 0.02
        inp['Wf'] = jax.random.normal(ks[7], (FUSED, FUSED), jnp.float32) * FUSED ** (-0.5)
        inp['bf'] = jax.random.normal(ks[8], (FUSED,), jnp.float32) * 0.02
        for i, p in enumerate(PRE):
            inp[f'idx{i}'] = jnp.asarray(hilbert_flat_indices(IMG // p), jnp.int32)
        return inp
    _L0_tok_all = _L0_tok_setup()
    _L0_tok_in = {k: v for k, v in _L0_tok_all.items() if k in ('W0', 'b0', 'W1', 'b1', 'W2', 'b2', 'Wf', 'bf', 'idx0', 'idx1', 'idx2')}
    del _L0_tok_all

    def _L0_attn_setup():
        import jax, jax.numpy as jnp
        import numpy as np
        from jax import lax
        H = 192
        I = 384
        N = 16
        R = 48
        K = 4
        NL = 16
        B, L = (2, 256)
        EPS = 1e-05

        def rmsnorm(x, w):
            return x * lax.rsqrt(jnp.mean(x * x, axis=-1, keepdims=True) + EPS) * w

        def causal_conv(u, w, b):
            uc = jnp.swapaxes(u, 1, 2)
            y = lax.conv_general_dilated(uc, w, (1,), [(K - 1, 0)], dimension_numbers=('NCH', 'OIH', 'NCH'), feature_group_count=I)
            return jnp.swapaxes(y + b[None, :, None], 1, 2)

        def selective_scan(u, dt, A, Bm, Cm, Dp):

            def step(h, inp):
                u_t, dt_t, B_t, C_t = inp
                dA = jnp.exp(dt_t[:, :, None] * A)
                h = dA * h + (dt_t * u_t)[:, :, None] * B_t[:, None, :]
                y = jnp.einsum('bin,bn->bi', h, C_t)
                return (h, y)
            inputs = tuple((jnp.moveaxis(a, 1, 0) for a in (u, dt, Bm, Cm)))
            h0 = jnp.zeros((u.shape[0],) + A.shape, u.dtype)
            _, ys = lax.scan(step, h0, inputs)
            return jnp.moveaxis(ys, 0, 1) + u * Dp

        def mamba_layer(x, p):
            in_w, cw, cb, xp_w, dtw, dtb, a_log, dp, ow, nw = p
            h = rmsnorm(x, nw)
            xz = jnp.einsum('blh,ch->blc', h, in_w)
            u, z = jnp.split(xz, 2, axis=-1)
            u = jax.nn.silu(causal_conv(u, cw, cb))
            proj = jnp.einsum('bli,ci->blc', u, xp_w)
            dt_r, Bm, Cm = (proj[..., :R], proj[..., R:R + N], proj[..., R + N:])
            dt = jax.nn.softplus(jnp.einsum('blr,ir->bli', dt_r, dtw) + dtb)
            A = -jnp.exp(a_log)
            y = selective_scan(u, dt, A, Bm, Cm, dp)
            y = y * jax.nn.silu(z)
            return x + jnp.einsum('bli,hi->blh', y, ow)
        key = jax.random.key(seed)
        ks = jax.random.split(key, 8)
        s = 0.02
        x = jax.random.normal(ks[0], (B, L, H), jnp.float32)
        in_proj_w = jax.random.normal(ks[1], (NL, 2 * I, H), jnp.float32) * s
        conv_w = jax.random.normal(ks[2], (NL, I, 1, K), jnp.float32) * 0.1
        conv_b = jnp.zeros((NL, I), jnp.float32)
        x_proj_w = jax.random.normal(ks[3], (NL, R + 2 * N, I), jnp.float32) * s
        dt_proj_w = jax.random.normal(ks[4], (NL, I, R), jnp.float32) * 0.01
        dt_proj_b = -4.0 + 0.1 * jax.random.normal(ks[5], (NL, I), jnp.float32)
        A_log = jnp.log(jnp.tile(jnp.arange(1, N + 1, dtype=jnp.float32), (NL, I, 1)))
        D = jnp.ones((NL, I), jnp.float32)
        out_proj_w = jax.random.normal(ks[6], (NL, H, I), jnp.float32) * s
        norm_w = jnp.ones((NL, H), jnp.float32)
        final_norm_w = jnp.ones((H,), jnp.float32)
        return {'x': x, 'in_proj_w': in_proj_w, 'conv_w': conv_w, 'conv_b': conv_b, 'x_proj_w': x_proj_w, 'dt_proj_w': dt_proj_w, 'dt_proj_b': dt_proj_b, 'A_log': A_log, 'D': D, 'out_proj_w': out_proj_w, 'norm_w': norm_w, 'final_norm_w': final_norm_w}
    _L0_attn_all = _L0_attn_setup()
    _L0_attn_in = {k: v for k, v in _L0_attn_all.items() if k in ('in_proj_w', 'conv_w', 'conv_b', 'x_proj_w', 'dt_proj_w', 'dt_proj_b', 'A_log', 'D', 'out_proj_w', 'norm_w', 'final_norm_w')}
    del _L0_attn_all

    def _L0_ffn_setup():
        import jax, jax.numpy as jnp
        import numpy as np
        NUM_EXPERT = 8
        TOP_K = 1
        key = jax.random.key(seed)
        ks = jax.random.split(key, 6)
        B, S, D, E, F = (8, 512, 192, 8, 469)
        scale = 0.02
        return {'x': jax.random.normal(ks[0], (B, S, D), dtype=jnp.float32), 'Wg': jax.random.normal(ks[1], (E, D), dtype=jnp.float32) * scale, 'bg': jnp.zeros((E,), dtype=jnp.float32), 'W1': jax.random.normal(ks[2], (E, F, D), dtype=jnp.float32) * scale, 'W2': jax.random.normal(ks[3], (E, F, D), dtype=jnp.float32) * scale, 'W3': jax.random.normal(ks[4], (E, D, F), dtype=jnp.float32) * scale}
    _L0_ffn_all = _L0_ffn_setup()
    _L0_ffn_in = {k: v for k, v in _L0_ffn_all.items() if k in ('Wg', 'bg', 'W1', 'W2', 'W3')}
    del _L0_ffn_all
    return {'x': x, 'cls_tok': cls_tok, 'L0_tok_W0': _L0_tok_in['W0'], 'L0_tok_b0': _L0_tok_in['b0'], 'L0_tok_W1': _L0_tok_in['W1'], 'L0_tok_b1': _L0_tok_in['b1'], 'L0_tok_W2': _L0_tok_in['W2'], 'L0_tok_b2': _L0_tok_in['b2'], 'L0_tok_Wf': _L0_tok_in['Wf'], 'L0_tok_bf': _L0_tok_in['bf'], 'L0_tok_idx0': _L0_tok_in['idx0'], 'L0_tok_idx1': _L0_tok_in['idx1'], 'L0_tok_idx2': _L0_tok_in['idx2'], 'L0_attn_in_proj_w': _L0_attn_in['in_proj_w'], 'L0_attn_conv_w': _L0_attn_in['conv_w'], 'L0_attn_conv_b': _L0_attn_in['conv_b'], 'L0_attn_x_proj_w': _L0_attn_in['x_proj_w'], 'L0_attn_dt_proj_w': _L0_attn_in['dt_proj_w'], 'L0_attn_dt_proj_b': _L0_attn_in['dt_proj_b'], 'L0_attn_A_log': _L0_attn_in['A_log'], 'L0_attn_D': _L0_attn_in['D'], 'L0_attn_out_proj_w': _L0_attn_in['out_proj_w'], 'L0_attn_norm_w': _L0_attn_in['norm_w'], 'L0_attn_final_norm_w': _L0_attn_in['final_norm_w'], 'L0_ffn_Wg': _L0_ffn_in['Wg'], 'L0_ffn_bg': _L0_ffn_in['bg'], 'L0_ffn_W1': _L0_ffn_in['W1'], 'L0_ffn_W2': _L0_ffn_in['W2'], 'L0_ffn_W3': _L0_ffn_in['W3']}

def reference(x, cls_tok, L0_tok_W0, L0_tok_b0, L0_tok_W1, L0_tok_b1, L0_tok_W2, L0_tok_b2, L0_tok_Wf, L0_tok_bf, L0_tok_idx0, L0_tok_idx1, L0_tok_idx2, L0_attn_in_proj_w, L0_attn_conv_w, L0_attn_conv_b, L0_attn_x_proj_w, L0_attn_dt_proj_w, L0_attn_dt_proj_b, L0_attn_A_log, L0_attn_D, L0_attn_out_proj_w, L0_attn_norm_w, L0_attn_final_norm_w, L0_ffn_Wg, L0_ffn_bg, L0_ffn_W1, L0_ffn_W2, L0_ffn_W3):
    import jax
    import jax.numpy as jnp

    def _L0_tok_ref(x, W0, b0, W1, b1, W2, b2, Wf, bf, idx0, idx1, idx2):
        import jax, jax.numpy as jnp
        import numpy as np
        B = 16
        IMG = 64
        CH = 3
        EMBED = 64
        GP = 16
        PRE = [1, 2, 4]
        N_LEVELS = 3
        FUSED = EMBED * N_LEVELS

        def hilbert_flat_indices(n):
            t = np.arange(n * n, dtype=np.int64)
            x = np.zeros(n * n, dtype=np.int64)
            y = np.zeros(n * n, dtype=np.int64)
            s = 1
            while s < n:
                rx = 1 & t // 2
                ry = 1 & (t ^ rx)
                swap = ry == 0
                flip = swap & (rx == 1)
                x = np.where(flip, s - 1 - x, x)
                y = np.where(flip, s - 1 - y, y)
                x2 = np.where(swap, y, x)
                y2 = np.where(swap, x, y)
                x, y = (x2, y2)
                x = x + s * rx
                y = y + s * ry
                t = t // 4
                s *= 2
            return y * n + x

        def _level(x, idx, W, b, p, gp):
            Bsz, C, H, _ = x.shape
            h = H // p
            t = x.reshape(Bsz, C, h, p, h, p).transpose(0, 2, 4, 3, 5, 1).reshape(Bsz, h * h, p * p * C)
            t = t[:, idx]
            t = t.reshape(Bsz, h * h // gp, gp * p * p * C)
            return t @ W.T + b

        def _interp_linear(x, n_out):
            L = x.shape[1]
            pos = (jnp.arange(n_out, dtype=jnp.float32) + 0.5) * (L / n_out) - 0.5
            pos = jnp.clip(pos, 0.0, L - 1)
            i0 = jnp.floor(pos).astype(jnp.int32)
            i1 = jnp.minimum(i0 + 1, L - 1)
            w = (pos - i0).astype(x.dtype)
            return x[:, i0] * (1.0 - w)[None, :, None] + x[:, i1] * w[None, :, None]
        Ws = [(idx0, W0, b0, PRE[0]), (idx1, W1, b1, PRE[1]), (idx2, W2, b2, PRE[2])]
        outs = [_level(x, idx, W, b, p, GP) for idx, W, b, p in Ws]
        n_tokens = outs[0].shape[1]
        outs = [outs[0]] + [_interp_linear(o, n_tokens) for o in outs[1:]]
        y = jnp.concatenate(outs, axis=-1)
        return y @ Wf.T + bf

    def _L0_attn_ref(x, in_proj_w, conv_w, conv_b, x_proj_w, dt_proj_w, dt_proj_b, A_log, D, out_proj_w, norm_w, final_norm_w):
        import jax, jax.numpy as jnp
        import numpy as np
        from jax import lax
        H = 192
        I = 384
        N = 16
        R = 48
        K = 4
        NL = 16
        B, L = (2, 256)
        EPS = 1e-05

        def rmsnorm(x, w):
            return x * lax.rsqrt(jnp.mean(x * x, axis=-1, keepdims=True) + EPS) * w

        def causal_conv(u, w, b):
            uc = jnp.swapaxes(u, 1, 2)
            y = lax.conv_general_dilated(uc, w, (1,), [(K - 1, 0)], dimension_numbers=('NCH', 'OIH', 'NCH'), feature_group_count=I)
            return jnp.swapaxes(y + b[None, :, None], 1, 2)

        def selective_scan(u, dt, A, Bm, Cm, Dp):

            def step(h, inp):
                u_t, dt_t, B_t, C_t = inp
                dA = jnp.exp(dt_t[:, :, None] * A)
                h = dA * h + (dt_t * u_t)[:, :, None] * B_t[:, None, :]
                y = jnp.einsum('bin,bn->bi', h, C_t)
                return (h, y)
            inputs = tuple((jnp.moveaxis(a, 1, 0) for a in (u, dt, Bm, Cm)))
            h0 = jnp.zeros((u.shape[0],) + A.shape, u.dtype)
            _, ys = lax.scan(step, h0, inputs)
            return jnp.moveaxis(ys, 0, 1) + u * Dp

        def mamba_layer(x, p):
            in_w, cw, cb, xp_w, dtw, dtb, a_log, dp, ow, nw = p
            h = rmsnorm(x, nw)
            xz = jnp.einsum('blh,ch->blc', h, in_w)
            u, z = jnp.split(xz, 2, axis=-1)
            u = jax.nn.silu(causal_conv(u, cw, cb))
            proj = jnp.einsum('bli,ci->blc', u, xp_w)
            dt_r, Bm, Cm = (proj[..., :R], proj[..., R:R + N], proj[..., R + N:])
            dt = jax.nn.softplus(jnp.einsum('blr,ir->bli', dt_r, dtw) + dtb)
            A = -jnp.exp(a_log)
            y = selective_scan(u, dt, A, Bm, Cm, dp)
            y = y * jax.nn.silu(z)
            return x + jnp.einsum('bli,hi->blh', y, ow)
        params = (in_proj_w, conv_w, conv_b, x_proj_w, dt_proj_w, dt_proj_b, A_log, D, out_proj_w, norm_w)

        def body(carry, p):
            return (mamba_layer(carry, p), None)
        out, _ = lax.scan(body, x, params)
        return rmsnorm(out, final_norm_w)

    def _L0_ffn_ref(x, Wg, bg, W1, W2, W3):
        import jax, jax.numpy as jnp
        import numpy as np
        NUM_EXPERT = 8
        TOP_K = 1
        B, S, D = x.shape
        E = Wg.shape[0]
        xf = x.reshape(B * S, D)
        gate = xf @ Wg.T + bg
        vals, idx = jax.lax.top_k(gate, TOP_K)
        probs = jax.nn.softmax(vals, axis=-1)
        dispatch = jnp.sum(jax.nn.one_hot(idx, E, dtype=x.dtype) * probs[..., None], axis=1)
        h = jax.nn.silu(jnp.einsum('td,efd->tef', xf, W1)) * jnp.einsum('td,efd->tef', xf, W2)
        out = jnp.einsum('tef,edf,te->td', h, W3, dispatch)
        return out.reshape(B, S, D)
    h = _L0_tok_ref(x, L0_tok_W0, L0_tok_b0, L0_tok_W1, L0_tok_b1, L0_tok_W2, L0_tok_b2, L0_tok_Wf, L0_tok_bf, L0_tok_idx0, L0_tok_idx1, L0_tok_idx2)
    h = jnp.concatenate([jnp.broadcast_to(cls_tok, (h.shape[0], 1, h.shape[2])), h], axis=1)
    h = h + _L0_attn_ref(_layernorm(h, axis=-1), L0_attn_in_proj_w, L0_attn_conv_w, L0_attn_conv_b, L0_attn_x_proj_w, L0_attn_dt_proj_w, L0_attn_dt_proj_b, L0_attn_A_log, L0_attn_D, L0_attn_out_proj_w, L0_attn_norm_w, L0_attn_final_norm_w)
    h = h + _L0_ffn_ref(_layernorm(h, axis=-1), L0_ffn_Wg, L0_ffn_bg, L0_ffn_W1, L0_ffn_W2, L0_ffn_W3)
    return h

_drawn_inputs = setup_inputs


def setup_inputs(seed=0):
    import zlib

    import numpy as np

    out = dict(_drawn_inputs(seed))
    spreads = {'L0_attn_conv_b': (0.0, 0.8),
     'L0_attn_D': (1.0, 0.6),
     'L0_attn_norm_w': (1.0, 0.6),
     'L0_attn_final_norm_w': (1.0, 0.2),
     'L0_ffn_bg': (0.0, 0.8)}
    factors = {'L0_tok_b0': 4.568,
     'L0_tok_b1': 4.597,
     'L0_tok_b2': 4.002,
     'L0_attn_in_proj_w': 7.484,
     'L0_attn_conv_w': 8.0,
     'L0_attn_x_proj_w': 8.0,
     'L0_attn_dt_proj_w': 8.0,
     'L0_attn_dt_proj_b': 8.0,
     'L0_attn_A_log': 8.0,
     'L0_attn_out_proj_w': 7.448,
     'L0_ffn_Wg': 6.851,
     'L0_ffn_W1': 6.394,
     'L0_ffn_W2': 6.331,
     'L0_ffn_W3': 6.302}
    for name, (base, spread) in spreads.items():
        noise = np.random.default_rng([zlib.crc32(name.encode()), seed]).standard_normal(out[name].shape)
        drawn = base * np.exp(spread * noise) if base else spread * noise
        out[name] = jnp.asarray(drawn.astype(out[name].dtype))
    for name, factor in factors.items():
        out[name] = (out[name] * factor).astype(out[name].dtype)
    return out
```

```python
import math
from contextlib import ExitStack

import concourse.bass as bass
from concourse import mybir

ALU = mybir.AluOpType
ACT = mybir.ActivationFunctionType
F32 = mybir.dt.float32
BF16 = mybir.dt.bfloat16
AX = mybir.AxisListType

B = 2
T = 257
TP = T - 1
H = 192
HP = 96
HK = H // HP
I = 384
IK = I // 128
N = 16
R = 48
KC = 4
NL = 16
EPS = 1e-5
NE = 8
F = 469
FK = (F + 127) // 128
FS = [min(128, F - 128 * k) for k in range(FK)]
GP = 16
EMB = 64
W3T = IK * T
NPRM = KC + 3 + N
HR = 4
LN_EXP = "natural_log_exp_and_others"
RING = 4
NW = 6
HS = B * NL
BD, BB, BY, BA = 0, 2, 4, 6

DVE_A = {3: ["gate"], 5: ["resid"], 8: ["newton", "xn"], 11: ["conv0"], 13: ["conv1"], 14: ["conv2"], 19: ["r1"],
         20: ["lo"], 26: ["clamp1"], 27: ["clamp2"], 28: ["dt"]}
ACT_A = {4: ["sq"], 5: ["rstd"], 6: ["evac0", "evac1"], 7: ["evac2", "evac3"], 8: ["evac4", "evac5"],
         9: ["silu"], 10: ["split", "uD"], 11: ["mid", "xpre"], 12: ["abs", "ex", "cc0", "cc1"],
         13: ["lnx", "cc2", "cc3", "cc4"], 14: [f"cc{n}" for n in range(5, 10)],
         15: [f"cc{n}" for n in range(10, 16)]}
PE_A = {2: ["outp"], 3: ["ss"], 4: ["inp0", "inp1"], 5: ["inp2", "inp3"], 6: ["inp4", "inp5"], 9: ["xproj"],
        11: ["dtp"], 12: ["cb0", "cb1", "cb2"], 13: ["cb3", "cb4"], 14: [f"cb{n}" for n in range(5, 10)],
        15: [f"cb{n}" for n in range(10, 16)]}
POOL_A = {12: ["bounds"], 15: ["dtu"]}


def mamba_vit(nc, P0, P1, P2, idx0, idx1, idx2, W0T, W1G, W2G, b0, b1, b2, WfT, bf, M1, M2, cls,
              in_wT, x_wT, dt_wT, out_wT, prm_d, norm_w, final_w, WgT, bg, E1, E2, E3, out):
    ctx = ExitStack()
    with ctx:
        def sb(name, shape, dt=F32):
            return ctx.enter_context(nc.sbuf_tensor(name, shape, dt))

        def sem(name):
            return ctx.enter_context(nc.semaphore(name))

        ps = ctx.enter_context(nc.psum_tensor("ps", [128, 8, 512], F32))
        flat = ps[:, :, :].rearrange("p b n -> p (b n)")

        ident = sb("ident", [128, 128])
        ones = sb("ones", [128, 128])
        sel = sb("sel", [96, 2 * N, 128], BF16)
        iota8 = sb("iota8", [128, NE])
        i0 = sb("i0", [128, 2, GP], mybir.dt.int32)
        i1 = sb("i1", [128, 8], mybir.dt.int32)
        i2 = sb("i2", [128, 2], mybir.dt.int32)
        G0 = sb("G0", [128, 2, GP, 6])
        G0b = sb("G0b", [128, 2, B, GP * 3])
        G1 = sb("G1", [128, 8, 24])
        G2 = sb("G2", [128, 2, 96])
        w0 = sb("w0", [48, EMB])
        b0c = sb("b0c", [EMB, 1])
        b1r = sb("b1r", [1, EMB])
        b2r = sb("b2r", [1, EMB])
        wf = sb("wf", [EMB, 3, H])
        bfc = sb("bfc", [HP, HK])
        tok1 = sb("tok1", [64, B, EMB])
        tok2 = sb("tok2", [16, B, EMB])
        h0 = sb("h0", [HP, HK, B, T])
        clsb = sb("clsb", [HP, HK])
        xs = [sb(f"xs{c}", [HP, HK, T]) for c in range(B)]
        sq = sb("sq", [HP, HK, T])
        lnv = sb("lnv", [HP, T])
        var = sb("var", [HP, T])
        root = sb("root", [HP, T])
        rootsq = sb("rootsq", [HP, T])
        rstd = sb("rstd", [HP, T])
        xn = sb("xn", [HP, HK, T])
        fw = sb("fw", [HP, HK])
        inw = [sb(f"inw{p}", [HP, HK, 2 * I]) for p in range(2)]
        xpw = [sb(f"xpw{p}", [128, IK, 96]) for p in range(2)]
        dtw = [sb(f"dtw{p}", [R, I]) for p in range(2)]
        outw = [sb(f"outw{p}", [128, IK, H]) for p in range(2)]
        prm = [sb(f"prm{p}", [128, IK, NPRM]) for p in range(2)]
        nw = [sb(f"nw{p}", [HP, HK]) for p in range(2)]
        expA = [sb(f"expA{p}", [128, IK, N]) for p in range(2)]
        negA = [sb(f"negA{p}", [128, IK, N]) for p in range(2)]
        uraw = sb("uraw", [128, IK, KC - 1 + T])
        uz = [sb(f"uz{c}", [128, 2 * IK, T]) for c in range(B)]
        dtr = sb("dtr", [R, T])
        bcs = [sb(f"bcs{c}", [96, T], BF16) for c in range(B)]
        bcr = sb("bcr", [64, T])
        xpre = sb("xpre", [128, W3T])
        absx = sb("absx", [128, W3T])
        ex = sb("ex", [128, W3T])
        e2h = sb("e2h", [128, W3T])
        e3t = sb("e3t", [128, W3T])
        mln = sb("mln", [128, 2])
        lnx = sb("lnx", [128, W3T])
        dt = [sb(f"dt{c}", [128, IK, T]) for c in range(B)]
        dtu = [sb(f"dtu{c}", [128, IK, T]) for c in range(B)]
        uD = [sb(f"uD{c}", [128, W3T]) for c in range(B)]
        cbc = [sb(f"cbc{c}", [128, N, T]) for c in range(B)]
        dA = sb("dA", [128, RING, IK, T])
        eps = sb("eps", [128, 1])
        hr = sb("hr", [128, RING, W3T])
        hc = sb("hc", [128, RING, W3T])
        gt = sb("gt", [128, IK, T])
        wg = sb("wg", [HP, HK, NE])
        bgr = sb("bgr", [1, NE])
        gate = sb("gate", [128, 5, NE])
        mx = sb("mx", [128, 5])
        eq = sb("eq", [128, 5, NE])
        cand = sb("cand", [128, 5, NE])
        first = sb("first", [128, 5])
        oneh = sb("oneh", [128, 5, NE])
        dif = sb("dif", [128, 5])
        prob = sb("prob", [128, 5])
        rden = sb("rden", [128, 5])
        pn = sb("pn", [128, 5])
        disp = sb("disp", [128, 5, NE], BF16)
        e1 = [sb(f"e1{p}", [HP, HK, F]) for p in range(2)]
        e2 = [sb(f"e2{p}", [HP, HK, F]) for p in range(2)]
        e3 = [sb(f"e3{p}", [128, FK, H]) for p in range(2)]
        dispT = sb("dispT", [NE, B * T], BF16)
        identb = sb("identb", [128, 128], BF16)

        def inside(buf, at, parts, **dims):
            names, n = " ".join(dims), 1
            for d in dims.values():
                n *= d
            v = buf[0:parts, at:at + n]
            sizes = dict(list(dims.items())[1:])
            return v.rearrange(f"p ({names}) -> p {names}", **sizes) if len(dims) > 1 else v

        cb0, cb1 = (cbc[c][:, :, :].rearrange("p n t -> p (n t)") for c in range(B))
        hcf = hc[:, :, :].rearrange("p r n -> p (r n)")
        hrf = hr[:, :, :].rearrange("p r n -> p (r n)")
        GT0 = inside(cb0, 0, 48, n=512)
        GT1 = inside(cb0, 512, 12, n=2048)
        GT2 = inside(cb0, 2560, 48, n=512)
        w1 = inside(cb0, 3072, 12, g=GP, e=EMB)
        w2 = inside(cb1, 0, 48, g=GP, e=EMB)
        cat = inside(cb1, 1024, EMB, l=3, n=512)
        m1 = inside(cb1, 2560, 64, n=256)
        m2 = inside(cb1, 2816, 16, n=256)
        xc = inside(hcf, 0, HP, k=HK, b=B, t=T)
        sq2 = inside(hcf, HK * B * T, HP, k=HK, b=B, t=T)
        lnv2 = inside(hcf, 2 * HK * B * T, HP, b=B, t=T)
        var2 = inside(hrf, 0, HP, b=B, t=T)
        root2 = inside(hrf, B * T, HP, b=B, t=T)
        rstd2 = inside(hcf, 2 * HK * B * T + B * T, HP, b=B, t=T)
        maskb = inside(cb0, 0, HP, e=NE, n=B * T)
        xm = [inside(cb1, p * HK * B * T, HP, k=HK, n=B * T) for p in range(2)]
        uzf = uz[0][:, :, :].rearrange("p k t -> p (k t)")
        hf = inside(uzf, 0, 128, r=HR, t=T)
        sg = inside(uzf, HR * T, 128, r=2, t=T)
        outT = inside(cb1, 2 * HK * B * T, HP, k=HK, b=B, t=T)
        outs = inside(hrf, 2 * B * T, 128, j=B * 3, h=H)

        block = ctx.enter_context(nc.Block())

        s_idx, s_tokw, s_cls = sem("s_idx"), sem("s_tokw"), sem("s_cls")
        s_zero, s_const = sem("s_zero"), sem("s_const")
        s_gather = sem("s_gather")
        s_gt, s_gtc, s_tokm, s_tokc, s_int, s_intc, s_fuse, s_h0 = (
            sem(n) for n in ("s_gt", "s_gtc", "s_tokm", "s_tokc", "s_int", "s_intc", "s_fuse", "s_h0"))
        s_sum, s_xc, s_sq2, s_ss2, s_ln2, s_rs2, s_lno = (
            sem(n) for n in ("s_sum", "s_xc", "s_sq2", "s_ss2", "s_ln2", "s_rs2", "s_lno"))
        s_w = [sem(f"s_w{p}") for p in range(2)]
        s_ow = [sem(f"s_ow{p}") for p in range(2)]
        names = ("s_gate s_outp s_resid s_sq s_ss s_ln s_rstd s_xn s_inp s_evac s_conv s_silu s_ud s_xproj "
                 "s_dtr s_hi s_r1 s_mid s_lo s_dtp s_xpre s_abs s_ex s_ser s_lnx s_lo12 s_clamp s_dt s_dtu "
                 "s_cb s_cc s_negA s_cself s_ctap s_rt s_gate0 s_root s_rootsq s_newton s_root2 s_rsq2 s_g0b s_resid2 s_disp s_dispT s_dispc s_mask s_maskc").split()
        (s_gate, s_outp, s_resid, s_sq, s_ss, s_ln, s_rstd, s_xn, s_inp, s_evac, s_conv, s_silu, s_ud, s_xproj,
         s_dtr, s_hi, s_r1, s_mid, s_lo, s_dtp, s_xpre, s_abs, s_ex, s_ser, s_lnx, s_lo12, s_clamp, s_dt, s_dtu,
         s_cb, s_cc, s_negA, s_cself, s_ctap, s_rt, s_gate0, s_root, s_rootsq, s_newton, s_root2, s_rsq2, s_g0b, s_resid2, s_disp, s_dispT, s_dispc, s_mask, s_maskc) = (sem(n) for n in names)
        s_bb, s_dA, s_bmul, s_scan, s_cmul, s_ys = (
            sem(n) for n in ("s_bb", "s_dA", "s_bmul", "s_scan", "s_cmul", "s_ys"))
        s_h1, s_gatem, s_route, s_prob, s_fw, s_few, s_xb, s_xmask, s_up, s_act, s_fmul, s_down = (
            sem(n) for n in ("s_h1", "s_gatem", "s_route", "s_prob", "s_fw", "s_few", "s_xb", "s_xmask", "s_up",
                             "s_act", "s_fmul", "s_down"))
        s_e = [sem(f"s_e{p}") for p in range(2)]
        s_outT, s_tr, s_outs, s_out = sem("s_outT"), sem("s_tr"), sem("s_outs"), sem("s_out")

        def cnt(k, st, steps, c=0):
            b4, off = st
            return b4 * k + (k * (off + steps) + c)

        def cnt4(k, st, off):
            b4, _ = st
            return b4 * (k // 4) + k * (off // 4 + 1)

        def known(st, n):
            return not isinstance(st[0], int) or st[0] + st[1] >= n

        def is_last(st):
            return isinstance(st[0], int) and st[0] + st[1] == HS - 1

        def steps_of(eng, half_step):
            half_step((0, 0), 0)
            with eng.Fori(0, HS - 4, 4) as b4:
                for off in range(1, 5):
                    half_step((b4, off), off)
            for off in range(1, 4):
                half_step((HS - 4, off), off)

        def known_expert(e, p):
            return not isinstance(e, int) or e + p >= 1

        def experts_of(eng, expert):
            for p in range(2):
                expert(0, p)
            with eng.Fori(1, NE // 2) as pair:
                for p in range(2):
                    expert(pair * 2, p)

        h0f = h0[:, :, :, :].rearrange("p k b t -> p k (b t)")
        xcf = xc[:, :, :, :].rearrange("p k b t -> p k (b t)")

        @block.sync
        def _(sp):
            sp.dma_start(i0[:, :, :], idx0).then_inc(s_idx, 16)
            sp.dma_start(i1[:, :], idx1).then_inc(s_idx, 16)
            sp.dma_start(i2[:, :], idx2).then_inc(s_idx, 16)
            for dst, src in ((w0[:, :], W0T), (w1[:, :, :], W1G), (w2[:, :, :], W2G),
                             (b0c[:, :], b0),
                             (b1r[:, :], b1.rearrange("(a n) -> a n", a=1)),
                             (b2r[:, :], b2.rearrange("(a n) -> a n", a=1)),
                             (wf[:, :, :], WfT.rearrange("(l p) o -> p l o", p=EMB)),
                             (bfc[:, :], bf),
                             (m1[:, :], M1), (m2[:, :], M2)):
                sp.dma_start(dst, src).then_inc(s_tokw, 16)
            sp.dma_start(clsb[:, :], cls).then_inc(s_cls, 16)

            def load_layer(lyr, p):
                sp.dma_start(inw[p][:, :, :], in_wT[lyr].rearrange("(k p) c -> p k c", p=HP)).then_inc(s_w[p], 16)
                x_w = x_wT[lyr].rearrange("(k p) c -> p k c", p=128)
                sp.dma_start(xpw[p][:, :, 0:R], x_w[:, :, 0:R]).then_inc(s_w[p], 16)
                sp.dma_start(xpw[p][:, :, 64:96], x_w[:, :, R:R + 2 * N]).then_inc(s_w[p], 16)
                sp.dma_start(dtw[p][:, :], dt_wT[lyr]).then_inc(s_w[p], 16)
                sp.dma_start(prm[p][:, :, :], prm_d[lyr].rearrange("(k p) c -> p k c", p=128)).then_inc(s_w[p], 16)
                sp.dma_start(nw[p][:, :], norm_w[lyr]).then_inc(s_w[p], 16)

            def load_out(lyr, p):
                sp.dma_start(outw[p][:, :, :], out_wT[lyr].rearrange("(k p) c -> p k c", p=128)).then_inc(s_ow[p], 16)

            for p in range(2):
                load_layer(p, p)
                load_out(p, p)
            for dst, src in ((fw[:, :], final_w),
                             (wg[:, :, :], WgT.rearrange("(k p) e -> p k e", p=HP)),
                             (bgr[:, :], bg.rearrange("(a n) -> a n", a=1))):
                sp.dma_start(dst, src).then_inc(s_fw, 16)

            def load_expert(e, p):
                sp.dma_start(e1[p][:, :, :], E1[e].rearrange("(k p) f -> p k f", p=HP)).then_inc(s_e[p], 16)
                sp.dma_start(e2[p][:, :, :], E2[e].rearrange("(k p) f -> p k f", p=HP)).then_inc(s_e[p], 16)
                sp.dma_start(e3[p][:, 0:FK - 1, :], E3[e, 0:128 * (FK - 1)].rearrange("(k p) d -> p k d", p=128))\
                  .then_inc(s_e[p], 16)
                sp.dma_start(e3[p][0:FS[-1], FK - 1, :], E3[e, 128 * (FK - 1):F]).then_inc(s_e[p], 16)

            for p in range(2):
                load_expert(p, p)
            with sp.Fori(0, NL // 2 - 1) as pair:
                l2 = pair * 2
                for p in range(2):
                    sp.wait_ge(s_xpre, l2 * (2 * IK) + 2 * IK * (p + 1))
                    load_layer(l2 + (p + 2), p)
                    sp.wait_ge(s_outp, l2 * (2 * HK) + 2 * HK * (p + 1))
                    load_out(l2 + (p + 2), p)
            with sp.Fori(0, NE // 2 - 1) as pair:
                e2l = pair * 2
                for p in range(2):
                    sp.wait_ge(s_down, e2l * (2 * FK) + 2 * FK * (p + 1))
                    load_expert(e2l + (p + 2), p)
            for b in range(B):
                for k, (t0, n) in enumerate(((0, 128), (128, 128), (256, 1))):
                    sp.wait_ge(s_outs, 3 * b + k + 1)
                    sp.dma_start(out[b, t0:t0 + n, :], outs[0:n, 3 * b + k, :]).then_inc(s_out, 16)
            sp.wait_ge(s_out, 16 * B * 3)

        @block.gpsimd
        def _(pool):
            pool.memset(ident[:, :], 0.0).then_inc(s_zero, 1)
            pool.memset(sel[:, :, :], 0.0).then_inc(s_zero, 1)
            pool.wait_ge(s_zero, 2)
            pool.affine_select(out=ident[:, :], in_=ident[:, :], compare_op=ALU.not_equal, fill=1.0, base=0,
                               pattern=[[-1, 128]], channel_multiplier=1).then_inc(s_const, 1)
            pool.wait_ge(s_idx, 48)
            pool.wait_ge(s_const, 1)
            for k in range(2):
                for g in range(GP):
                    pool.indirect_dma_start(out=G0[:, k, g, :], out_offset=None, in_=P0[:, :],
                                            in_offset=bass.IndirectOffsetOnAxis(ap=i0[:, k, g:g + 1], axis=0))\
                        .then_inc(s_gather, 16)
            for q in range(8):
                pool.indirect_dma_start(out=G1[:, q, :], out_offset=None, in_=P1[:, :],
                                        in_offset=bass.IndirectOffsetOnAxis(ap=i1[:, q:q + 1], axis=0))\
                    .then_inc(s_gather, 16)
            for q in range(2):
                pool.indirect_dma_start(out=G2[:, q, :], out_offset=None, in_=P2[:, :],
                                        in_offset=bass.IndirectOffsetOnAxis(ap=i2[:, q:q + 1], axis=0))\
                    .then_inc(s_gather, 16)
            pool.wait_ge(s_gather, 16 * 42)
            for j in range(3):
                blk = sel[32 * j:32 * j + 32, :, :]
                pool.affine_select(out=blk, in_=blk, compare_op=ALU.not_equal, fill=1.0, base=0,
                                   pattern=[[-1, 2 * N], [0, 128]], channel_multiplier=1).then_inc(s_const, 1)
                pool.wait_ge(s_const, 2 + j)
            pool.iota(iota8[:, :], pattern=[[1, NE]], base=-NE, channel_multiplier=0,
                      allow_small_or_imprecise_dtypes=True).then_inc(s_const, 1)

            def phase_a(st, items):
                c = (st[1]) % 2
                if "bounds" in items:
                    pool.wait_ge(s_ex, cnt(1, st, 1))
                    pool.wait_ge(s_ser, cnt(2, st, 0, 1))
                    pool.tensor_tensor(e2h[:, :], ex[:, :], e2h[:, :], ALU.subtract).then_inc(s_lo12, 1)
                    pool.wait_ge(s_ser, cnt(2, st, 1))
                    pool.wait_ge(s_lo12, cnt(2, st, 0, 1))
                    pool.tensor_tensor(e3t[:, :], e2h[:, :], e3t[:, :], ALU.add).then_inc(s_lo12, 1)
                if "dtu" in items:
                    pool.wait_ge(s_dt, cnt(1, st, 1))
                    pool.wait_ge(s_silu, cnt(1, st, 1))
                    pool.tensor_tensor(dtu[c][:, :, :], dt[c][:, :, :], uz[c][:, 0:IK, :], ALU.mult)\
                        .then_inc(s_dtu, 1)

            def half_step(st, off):
                c = off % 2
                nxt = (st[0], off + 1)
                last = is_last(st)
                for n in range(N):
                    pool.wait_ge(s_scan, cnt(N, st, 0, n + 1))
                    pool.wait_ge(s_cc, cnt(N, st, 0, n + 1))
                    if n >= RING or known(st, 1):
                        pool.wait_ge(s_ys, cnt(N, st, 0, n - RING + 1))
                    pool.tensor_tensor(hc[:, n % RING, :].rearrange("p (k t) -> p k t", k=IK),
                                       hr[:, n % RING, :].rearrange("p (k t) -> p k t", k=IK),
                                       cbc[c][:, n:n + 1, :].broadcast_to([128, IK, T]), ALU.mult)\
                        .then_inc(s_cmul, 1)
                    if not last:
                        phase_a(nxt, POOL_A.get(n, ()))

            phase_a((0, 0), ("bounds", "dtu"))
            steps_of(pool, half_step)

            def masked(e, p):
                pool.wait_ge(s_maskc, e + (p + 1))
                for k in range(HK):
                    ins = pool.tensor_tensor(xm[p][:, k, :], xcf[:, k, :], maskb[:, bass.ds(e + p, 1), :]
                                             .rearrange("p a t -> p (a t)"), ALU.mult)
                ins.then_inc(s_xmask, 1)

            pool.wait_ge(s_lno, 4)
            for p in range(2):
                masked(0, p)
            with pool.Fori(1, NE // 2) as pair:
                e = pair * 2
                for p in range(2):
                    pool.wait_ge(s_up, e * (2 * FK) + 2 * FK * (p - 1))
                    masked(e, p)

        @block.scalar
        def _(act):
            A = act.activation
            act.wait_ge(s_gt, 1)
            A(GT0[:, :], ps[0:48, 0, :], ACT.Copy).then_inc(s_gtc, 1)
            A(GT2[:, :], ps[0:48, 5, :], ACT.Copy).then_inc(s_gtc, 1)
            act.wait_ge(s_tokw, 160)
            act.wait_ge(s_tokm, 1)
            A(cat[:, 0, :], ps[0:EMB, 6, :], ACT.Identity, bias=b0c[:, :]).then_inc(s_tokc, 1)
            act.wait_ge(s_tokm, 2)
            A(tok1[:, :, :], ps[0:64, 7, 0:128].rearrange("p (b e) -> p b e", b=B), ACT.Copy).then_inc(s_tokc, 1)
            A(tok2[:, :, :], ps[0:16, 7, 128:256].rearrange("p (b e) -> p b e", b=B), ACT.Copy).then_inc(s_tokc, 1)
            act.wait_ge(s_int, 1)
            A(cat[:, 1:3, :], ps[0:EMB, 0:2, :], ACT.Copy).then_inc(s_intc, 1)
            act.wait_ge(s_fuse, 1)
            for k in range(HK):
                A(h0[:, k, :, 1:T], ps[0:HP, 2 + k, :].rearrange("p (b t) -> p b t", b=B), ACT.Identity,
                  bias=bfc[:, k:k + 1]).then_inc(s_h0, 1)
            act.wait_ge(s_cls, 16)
            for b in range(B):
                A(h0[:, :, b, 0], clsb[:, :], ACT.Copy).then_inc(s_h0, 1)

            def layer_norm(r):
                act.wait_ge(s_xc, B * (r // 2 + 1))
                A(sq2[:, :, :, :].rearrange("p k b t -> p (k b t)"), xc[:, :, :, :].rearrange("p k b t -> p (k b t)"),
                  ACT.Square).then_inc(s_sq2, 1)
                inverse_root(r)

            def inverse_root(r):
                act.wait_ge(s_ss2, r + 1)
                A(var2[:, :, :], ps[0:HP, 2:4, 0:T], ACT.Identity, bias=eps[0:HP, :], scale=1.0 / H)
                A(lnv2[:, :, :], ps[0:HP, 2:4, 0:T], ACT.Ln, bias=eps[0:HP, :], scale=1.0 / H).then_inc(s_ln2, 1)
                act.wait_ge(s_ln2, r + 1)
                A(root2[:, :, :], lnv2[:, :, :], ACT.Exp, scale=-0.5).then_inc(s_root2, 1)
                act.wait_ge(s_root2, r + 1)
                A(lnv2[:, :, :], root2[:, :, :], ACT.Square).then_inc(s_rsq2, 1)

            act.preload_act_table_set(LN_EXP)
            act.wait_ge(s_cself, 4)
            layer_norm(0)

            def phase_a(st, items):
                off = st[1]
                c = off % 2
                p = (off // 2) % 2
                for it in items:
                    if it == "sq":
                        if known(st, 2):
                            act.wait_ge(s_resid, cnt(HK, st, -1))
                        else:
                            act.wait_ge(s_lno, 2)
                        A(sq[:, :, :], xs[c][:, :, :], ACT.Square).then_inc(s_sq, 1)
                        if off % 2 == 0:
                            act.wait_ge(s_w[p], cnt4(16 * NW, st, off))
                            A(expA[p][:, :, :], prm[p][:, :, KC + 3:NPRM], ACT.Exp).then_inc(s_negA, 1)
                    if it == "rstd":
                        if off % 2 == 0:
                            act.wait_ge(s_negA, cnt(1, st, 1))
                            A(negA[p][:, :, :], expA[p][:, :, :], ACT.Copy, scale=-1.0).then_inc(s_negA, 1)
                        act.wait_ge(s_ss, cnt(1, st, 1))
                        A(var[:, :], ps[0:HP, BA, 0:T], ACT.Identity, bias=eps[0:HP, :], scale=1.0 / H)
                        A(lnv[:, :], ps[0:HP, BA, 0:T], ACT.Ln, bias=eps[0:HP, :], scale=1.0 / H).then_inc(s_ln, 1)
                        act.wait_ge(s_ln, cnt(1, st, 1))
                        A(root[:, :], lnv[:, :], ACT.Exp, scale=-0.5).then_inc(s_root, 1)
                        act.wait_ge(s_root, cnt(1, st, 1))
                        A(rootsq[:, :], root[:, :], ACT.Square).then_inc(s_rootsq, 1)
                    if it[:4] == "evac":
                        m = int(it[4:])
                        act.wait_ge(s_inp, cnt(2 * IK, st, 0, m + 1))
                        bank = BA + (m + 1) % 2
                        if m < IK:
                            if known(st, 1):
                                act.wait_ge(s_conv, cnt(IK, st, 0))
                            A(uraw[:, m, KC - 1:], ps[:, bank, 0:T], ACT.Copy).then_inc(s_evac, 1)
                        else:
                            A(uz[c][:, m, :], ps[:, bank, 0:T], ACT.Copy).then_inc(s_evac, 1)
                    if it == "silu":
                        act.wait_ge(s_conv, cnt(IK, st, 1))
                        act.wait_ge(s_evac, cnt(2 * IK, st, 1))
                        A(uz[c][:, :, :], uz[c][:, :, :], ACT.Silu).then_inc(s_silu, 1)
                        act.preload_act_table_set(LN_EXP)
                    if it == "split":
                        act.wait_ge(s_xproj, cnt(1, st, 1))
                        A(dtr[:, :], ps[0:R, BA + 1, 0:T], ACT.Copy).then_inc(s_dtr, 1)
                        A(bcs[c][0:32, :], ps[64:96, BA + 1, 0:T], ACT.Copy).then_inc(s_hi, 1)
                    if it == "uD":
                        act.wait_ge(s_silu, cnt(1, st, 1))
                        for k in range(IK):
                            A(uD[c][:, k * T:(k + 1) * T], uz[c][:, k, :], ACT.Copy,
                              scale=prm[p][:, k, KC + 2:KC + 3]).then_inc(s_ud, 1)
                    if it == "mid":
                        act.wait_ge(s_r1, cnt(1, st, 1))
                        A(bcs[c][32:64, :], bcr[32:64, :], ACT.Copy).then_inc(s_mid, 1)
                    if it == "xpre":
                        if known(st, 1):
                            act.wait_ge(s_dt, cnt(1, st, 0))
                        for m in range(IK):
                            act.wait_ge(s_dtp, cnt(IK, st, 0, m + 1))
                            A(xpre[:, m * T:(m + 1) * T], ps[:, BA + m % 2, 0:T], ACT.Identity,
                              bias=prm[p][:, m, KC + 1:KC + 2]).then_inc(s_xpre, 1)
                    if it == "abs":
                        act.wait_ge(s_xpre, cnt(IK, st, 1))
                        A(absx[:, :], xpre[:, :], ACT.Abs).then_inc(s_abs, 1)
                    if it == "ex":
                        act.wait_ge(s_abs, cnt(1, st, 1))
                        A(ex[:, :], absx[:, :], ACT.Exp, scale=-1.0).then_inc(s_ex, 1)
                    if it == "lnx":
                        act.wait_ge(s_ex, cnt(1, st, 1))
                        A(e2h[:, :], absx[:, :], ACT.Exp, scale=-2.0, bias=mln[:, 0:1]).then_inc(s_ser, 1)
                        A(e3t[:, :], absx[:, :], ACT.Exp, scale=-3.0, bias=mln[:, 1:2]).then_inc(s_ser, 1)
                        A(lnx[:, :], ex[:, :], ACT.Ln, bias=ones[:, 0:1]).then_inc(s_lnx, 1)
                    if it[:2] == "cc":
                        n = int(it[2:])
                        act.wait_ge(s_cb, cnt(N, st, 0, n + 1))
                        A(cbc[c][:, n, :], ps[:, BA + n % 2, 0:T], ACT.Copy).then_inc(s_cc, 1)

            def half_step(st, off):
                c = off % 2
                p = (off // 2) % 2
                nxt = (st[0], off + 1)
                last = is_last(st)
                for n in range(N):
                    if n == 0:
                        act.wait_ge(s_dt, cnt(1, st, 1))
                        act.wait_ge(s_negA, cnt(1, st, 1 + (off + 1) % 2))
                    if n >= RING or known(st, 1):
                        act.wait_ge(s_scan, cnt(N, st, 0, n - RING + 1))
                    elif n == 0:
                        act.wait_ge(s_cself, 2)
                    for k in range(IK):
                        ins = A(dA[:, n % RING, k, 1:T], dt[c][:, k, 1:T], ACT.Exp, scale=negA[p][:, k, n:n + 1])
                    ins.then_inc(s_dA, 1)
                    if not last:
                        phase_a(nxt, ACT_A.get(n, ()))

            phase_a((0, 0), sum(ACT_A.values(), []))
            steps_of(act, half_step)

            act.wait_ge(s_resid, HK * HS)
            for c in range(B):
                ins = A(sq2[:, :, c, :], xs[c][:, :, :], ACT.Square)
            ins.then_inc(s_sq2, 1)
            inverse_root(1)
            layer_norm(2)
            act.wait_ge(s_route, 2)
            A(prob[:, :], dif[:, :], ACT.Exp).then_inc(s_prob, 1)

            def expert(e, p):
                for j in range(B * FK):
                    n = FS[j // B]
                    act.wait_ge(s_up, e * (B * FK) + (B * FK * p + j + 1))
                    if known_expert(e, p) or j >= 2:
                        act.wait_ge(s_fmul, e * (B * FK) + (B * FK * p + j - 1))
                    A(sg[0:n, j % 2, :], ps[0:n, 2 * (j % 2), 0:T], ACT.Silu).then_inc(s_act, 1)

            experts_of(act, expert)
            act.wait_ge(s_resid2, 1)
            for k in range(HK):
                A(outT[:, k, :, :], ps[0:HP, 4 + 2 * k:6 + 2 * k, 0:T], ACT.Copy).then_inc(s_outT, 1)
            for b in range(B):
                for k, n in enumerate((128, 128, 1)):
                    j = 3 * b + k
                    act.wait_ge(s_tr, j + 1)
                    A(outs[0:n, j, :], ps[0:n, j % 4, 0:H], ACT.Copy).then_inc(s_outs, 1)

        @block.vector
        def _(dve):
            V = nc.vector
            V.memset(ones[:, :], 1.0).then_inc(s_cself, 1)
            V.memset(dA[:, :, :, 0:1], 0.0).then_inc(s_cself, 1)
            V.memset(uraw[:, :, 0:KC - 1], 0.0).then_inc(s_cself, 1)
            V.memset(mln[:, 0:1], -math.log(2.0))
            V.memset(mln[:, 1:2], -math.log(3.0))
            V.memset(eps[:, :], EPS).then_inc(s_cself, 1)
            for p in range(2):
                V.memset(xpw[p][:, :, R:64], 0.0).then_inc(s_cself, 1)
            dve.wait_ge(s_gather, 16 * 42)
            for b in range(B):
                V.tensor_copy(G0b[:, :, b, :].rearrange("p k (g c) -> p k g c", c=3), G0[:, :, :, 3 * b:3 * b + 3])\
                    .then_inc(s_g0b, 1)
            dve.wait_ge(s_gt, 1)
            for b in range(B):
                V.tensor_copy(GT1[:, b * 1024:(b + 1) * 1024], flat[0:12, (1 + 2 * b) * 512:(3 + 2 * b) * 512])\
                    .then_inc(s_gtc, 1)

            def centre(r, src, srck):
                for b in range(B):
                    dve.wait_ge(s_sum, B * r + b + 1)
                    for k in range(HK):
                        ins = V.scalar_tensor_tensor(out=xc[:, k, b, :], in0=ps[0:HP, b, 0:T], scalar=-1.0 / H,
                                                     in1=src[:, k, b, :], op0=ALU.mult, op1=ALU.add)
                    ins.then_inc(s_xc, 1)

            def newton2(r):
                dve.wait_ge(s_rsq2, r + 1)
                V.scalar_tensor_tensor(out=var2[:, :, :], in0=lnv2[:, :, :], scalar=-0.5, in1=var2[:, :, :],
                                       op0=ALU.mult, op1=ALU.mult).then_inc(s_rs2, 1)
                dve.wait_ge(s_rs2, 2 * r + 1)
                V.scalar_tensor_tensor(out=rstd2[:, :, :], in0=var2[:, :, :], scalar=1.5, in1=root2[:, :, :],
                                       op0=ALU.add, op1=ALU.mult).then_inc(s_rs2, 1)
                dve.wait_ge(s_rs2, 2 * r + 2)

            dve.wait_ge(s_h0, 4)
            centre(0, h0, 0)
            newton2(0)
            dve.wait_ge(s_xc, 2)
            for c in range(B):
                V.tensor_tensor(xs[c][:, :, :], xc[:, :, c, :],
                                rstd2[:, c:c + 1, :].broadcast_to([HP, HK, T]), ALU.mult).then_inc(s_lno, 1)

            def phase_a(st, items):
                off = st[1]
                c = off % 2
                p = (off // 2) % 2
                for it in items:
                    if it == "gate" and known(st, 2):
                        dve.wait_ge(s_ys, cnt(N, st, -1))
                        V.tensor_tensor(gt[:, :, :].rearrange("p k t -> p (k t)"), flat[:, BY * 512:BY * 512 + W3T],
                                        uz[c][:, IK:2 * IK, :].rearrange("p k t -> p (k t)"), ALU.mult)\
                            .then_inc(s_gate, 1)
                    if it == "resid" and known(st, 2):
                        for k in range(HK):
                            dve.wait_ge(s_outp, cnt(HK, st, -2, k + 1))
                            V.tensor_tensor(xs[c][:, k, :], ps[0:HP, BA + k, 0:T], xs[c][:, k, :], ALU.add)\
                                .then_inc(s_resid, 1)
                    if it == "newton":
                        dve.wait_ge(s_rootsq, cnt(1, st, 1))
                        V.scalar_tensor_tensor(out=lnv[:, :], in0=rootsq[:, :], scalar=-0.5, in1=var[:, :],
                                               op0=ALU.mult, op1=ALU.mult).then_inc(s_newton, 1)
                        dve.wait_ge(s_newton, cnt(1, st, 1))
                        V.scalar_tensor_tensor(out=rstd[:, :], in0=lnv[:, :], scalar=1.5, in1=root[:, :],
                                               op0=ALU.add, op1=ALU.mult).then_inc(s_rstd, 1)
                    if it == "xn":
                        dve.wait_ge(s_rstd, cnt(1, st, 1))
                        dve.wait_ge(s_w[p], cnt4(16 * NW, st, off))
                        if known(st, 1):
                            dve.wait_ge(s_inp, cnt(2 * IK, st, 0))
                        for k in range(HK):
                            ins = V.scalar_tensor_tensor(out=xn[:, k, :], in0=xs[c][:, k, :], scalar=nw[p][:, k:k + 1],
                                                         in1=rstd[:, :], op0=ALU.mult, op1=ALU.mult)
                        ins.then_inc(s_xn, 1)
                    if it[:4] == "conv":
                        m = int(it[4:])
                        dve.wait_ge(s_evac, cnt(2 * IK, st, 0, m + 1))
                        V.tensor_scalar(uz[c][:, m, :], uraw[:, m, KC - 1:KC - 1 + T], prm[p][:, m, KC - 1:KC],
                                        prm[p][:, m, KC:KC + 1], ALU.mult, ALU.add).then_inc(s_ctap, 1)
                        for j in range(KC - 1):
                            dve.wait_ge(s_ctap, cnt(IK * (KC - 1), st, 0, m * (KC - 1) + j + 1))
                            V.scalar_tensor_tensor(out=uz[c][:, m, :], in0=uraw[:, m, j:j + T],
                                                   scalar=prm[p][:, m, j:j + 1], in1=uz[c][:, m, :],
                                                   op0=ALU.mult, op1=ALU.add)\
                                .then_inc(s_conv if j == KC - 2 else s_ctap, 1)
                    if it == "r1":
                        dve.wait_ge(s_hi, cnt(1, st, 1))
                        V.tensor_tensor(bcr[32:64, :], ps[64:96, BA + 1, 0:T], bcs[c][0:32, :], ALU.subtract)\
                            .then_inc(s_r1, 1)
                    if it == "lo":
                        dve.wait_ge(s_mid, cnt(1, st, 1))
                        V.tensor_tensor(bcs[c][64:96, :], bcr[32:64, :], bcs[c][32:64, :], ALU.subtract)\
                            .then_inc(s_lo, 1)
                    if it == "clamp1":
                        dve.wait_ge(s_lnx, cnt(1, st, 1))
                        dve.wait_ge(s_lo12, cnt(2, st, 0, 1))
                        V.tensor_tensor(lnx[:, :], lnx[:, :], e2h[:, :], ALU.max).then_inc(s_clamp, 1)
                    if it == "clamp2":
                        dve.wait_ge(s_clamp, cnt(2, st, 0, 1))
                        dve.wait_ge(s_lo12, cnt(2, st, 1))
                        V.tensor_tensor(lnx[:, :], lnx[:, :], e3t[:, :], ALU.min).then_inc(s_clamp, 1)
                    if it == "dt":
                        dve.wait_ge(s_clamp, cnt(2, st, 1))
                        V.scalar_tensor_tensor(out=dt[c][:, :, :].rearrange("p k t -> p (k t)"), in0=xpre[:, :],
                                               scalar=0.0, in1=lnx[:, :], op0=ALU.max, op1=ALU.add)\
                            .then_inc(s_dt, 1)

            def half_step(st, off):
                c = off % 2
                nxt = (st[0], off + 1)
                last = is_last(st)
                dbu = flat[:, BD * 512:BD * 512 + W3T]

                def a_items(q):
                    phase_a(nxt, [x for x in DVE_A.get(q, ()) if not last or x in ("gate", "resid")])

                for n in range(N):
                    if n == 0:
                        dve.wait_ge(s_dtu, cnt(1, st, 1))
                    dve.wait_ge(s_bb, cnt(N, st, 0, n + 1))
                    if n or known(st, 1):
                        dve.wait_ge(s_scan, cnt(N, st, 0, n))
                    V.tensor_tensor(dbu.rearrange("p (k t) -> p k t", k=IK), dtu[c][:, :, :],
                                    ps[:, BB + n % 2, 0:T].rearrange("p (a t) -> p a t", a=1)
                                    .broadcast_to([128, IK, T]), ALU.mult).then_inc(s_bmul, 1)
                    a_items(2 * n)
                    dve.wait_ge(s_dA, cnt(N, st, 0, n + 1))
                    dve.wait_ge(s_bmul, cnt(N, st, 0, n + 1))
                    if n >= RING or known(st, 1):
                        dve.wait_ge(s_cmul, cnt(N, st, 0, n - RING + 1))
                    V.tensor_tensor_scan(hr[:, n % RING, :], dA[:, n % RING, :, :].rearrange("p k t -> p (k t)"),
                                         dbu, 0.0, ALU.mult, ALU.add).then_inc(s_scan, 1)
                    a_items(2 * n + 1)

            for s in DVE_A.values():
                phase_a((0, 0), s)
            steps_of(dve, half_step)
            phase_a((HS - 4, 5), ("gate", "resid"))

            newton2(1)
            dve.wait_ge(s_fw, 48)
            for c in range(B):
                for k in range(HK):
                    V.scalar_tensor_tensor(out=xc[:, k, c, :], in0=xs[c][:, k, :], scalar=fw[:, k:k + 1],
                                           in1=rstd2[:, c, :], op0=ALU.mult, op1=ALU.mult).then_inc(s_h1, 1)
            dve.wait_ge(s_h1, B * HK)
            V.tensor_tensor(h0[:, :, :, :].rearrange("p k b t -> p (k b t)"),
                            h0[:, :, :, :].rearrange("p k b t -> p (k b t)"),
                            xc[:, :, :, :].rearrange("p k b t -> p (k b t)"), ALU.add).then_inc(s_h1, 1)
            dve.wait_ge(s_h1, B * HK + 1)
            centre(1, h0, 0)
            newton2(2)
            dve.wait_ge(s_xc, 4)
            for k in range(HK):
                V.tensor_tensor(xcf[:, k, :], xcf[:, k, :], rstd2[:, :, :].rearrange("p b t -> p (b t)"),
                                ALU.mult).then_inc(s_lno, 1)
            V.memset(gate[:, :, :], 0.0).then_inc(s_gate0, 1)
            V.tensor_copy(identb[:, :], ident[:, :]).then_inc(s_gate0, 1)
            dve.wait_ge(s_gatem, 1)
            dve.wait_ge(s_gate0, 2)
            V.tensor_copy(gate[:, 0:4, :], ps[:, 4, 0:4 * NE].rearrange("p (j e) -> p j e", j=4))
            V.tensor_copy(gate[0:2, 4:5, :], ps[0:2, 4, 4 * NE:5 * NE].rearrange("p (j e) -> p j e", j=1))\
                .then_inc(s_rt, 1)
            dve.wait_ge(s_rt, 1)
            V.tensor_reduce(mx[:, :], gate[:, :, :], AX.X, ALU.max).then_inc(s_route, 1)
            dve.wait_ge(s_route, 1)
            V.tensor_tensor(dif[:, :], mx[:, :], mx[:, :], ALU.subtract).then_inc(s_route, 1)
            V.tensor_tensor(eq[:, :, :], gate[:, :, :], mx[:, :].rearrange("p (j a) -> p j a", a=1)
                            .broadcast_to([128, 5, NE]), ALU.is_ge).then_inc(s_rt, 1)
            dve.wait_ge(s_rt, 2)
            dve.wait_ge(s_const, 5)
            io = iota8[:, :].rearrange("p (a e) -> p a e", a=1).broadcast_to([128, 5, NE])
            V.tensor_tensor(cand[:, :, :], eq[:, :, :], io, ALU.mult).then_inc(s_rt, 1)
            dve.wait_ge(s_rt, 3)
            V.tensor_reduce(first[:, :], cand[:, :, :], AX.X, ALU.min).then_inc(s_rt, 1)
            dve.wait_ge(s_rt, 4)
            V.tensor_tensor(oneh[:, :, :], io, first[:, :].rearrange("p (j a) -> p j a", a=1)
                            .broadcast_to([128, 5, NE]), ALU.is_equal).then_inc(s_rt, 1)
            dve.wait_ge(s_prob, 1)
            V.reciprocal(rden[:, :], prob[:, :]).then_inc(s_rt, 1)
            dve.wait_ge(s_rt, 6)
            V.tensor_tensor(pn[:, :], prob[:, :], rden[:, :], ALU.mult).then_inc(s_rt, 1)
            dve.wait_ge(s_rt, 7)
            V.tensor_tensor(disp[:, :, :], oneh[:, :, :], pn[:, :].rearrange("p (j a) -> p j a", a=1)
                            .broadcast_to([128, 5, NE]), ALU.mult).then_inc(s_disp, 1)

            dve.wait_ge(s_dispT, 1)
            V.tensor_copy(dispT[:, :], flat[0:NE, 2 * 512:2 * 512 + B * T]).then_inc(s_dispc, 1)
            for e in range(NE):
                dve.wait_ge(s_mask, e + 1)
                q = 2 * (e % 2)
                V.tensor_copy(maskb[:, e, :].rearrange("p (b t) -> p b t", b=B), ps[0:HP, q:q + 2, 0:T])\
                    .then_inc(s_maskc, 1)

            def expert(e, p):
                for j in range(B * FK):
                    n = FS[j // B]
                    dve.wait_ge(s_act, e * (B * FK) + (B * FK * p + j + 1))
                    if known_expert(e, p) or j >= HR:
                        dve.wait_ge(s_down, e * (B * FK) + (B * FK * p + j - HR + 1))
                    V.tensor_tensor(hf[0:n, j % HR, :], ps[0:n, 2 * (j % 2) + 1, 0:T], sg[0:n, j % 2, :], ALU.mult)\
                        .then_inc(s_fmul, 1)

            experts_of(dve, expert)

        @block.tensor
        def _(pe):
            M = pe.matmul
            pe.wait_ge(s_gather, 16 * 42)
            pe.wait_ge(s_g0b, B)
            pe.wait_ge(s_const, 1)
            for k in range(2):
                for b in range(B):
                    pe.transpose(ps[0:48, 0, b * 256 + k * 128:b * 256 + (k + 1) * 128], G0b[:, k, b, :],
                                 ident[:, :])
                    pe.transpose(ps[0:48, 5, b * 256 + k * 128:b * 256 + (k + 1) * 128],
                                 G2[:, k, 48 * b:48 * b + 48], ident[:, :])
            for q in range(8):
                for b in range(B):
                    c0 = (1 + 2 * b) * 512 + q * 128
                    ins = pe.transpose(flat[0:12, c0:c0 + 128], G1[:, q, 12 * b:12 * b + 12], ident[:, :])
            ins.then_inc(s_gt, 1)
            pe.wait_ge(s_gtc, 4)
            pe.wait_ge(s_tokw, 160)
            pe.wait_ge(s_cself, 1)
            M(ps[0:EMB, 6, :], w0[:, :], GT0[:, :], start=True, stop=True).then_inc(s_tokm, 1)
            for lvl, n, gt_, w_, br, c0 in ((1, 64, GT1, w1, b1r, 0), (2, 16, GT2, w2, b2r, 128)):
                for b in range(B):
                    o = ps[0:n, 7, c0 + b * EMB:c0 + (b + 1) * EMB]
                    for g in range(GP):
                        M(o, gt_[:, b * n * GP + g:(b + 1) * n * GP:GP], w_[:, g, :], start=(g == 0), stop=False)
                    ins = M(o, ones[0:1, 0:n], br[:, :], start=False, stop=True)
            ins.then_inc(s_tokm, 1)
            pe.wait_ge(s_tokc, 3)
            for b in range(B):
                M(ps[0:EMB, 0, b * 256:(b + 1) * 256], tok1[:, b, :], m1[:, :], start=True, stop=True)
                ins = M(ps[0:EMB, 1, b * 256:(b + 1) * 256], tok2[:, b, :], m2[:, :], start=True, stop=True)
            ins.then_inc(s_int, 1)
            pe.wait_ge(s_intc, 1)
            for k in range(HK):
                for lvl in range(3):
                    ins = M(ps[0:HP, 2 + k, :], wf[:, lvl, k * HP:(k + 1) * HP], cat[:, lvl, :],
                            start=(lvl == 0), stop=(lvl == 2))
            ins.then_inc(s_fuse, 1)

            def over_features(bank, src, b):
                for k in range(HK):
                    ins = M(ps[0:HP, bank, 0:T], ones[0:HP, 0:HP], src[:, k, b, :], start=(k == 0), stop=(k == HK - 1))
                return ins

            def squares(r):
                pe.wait_ge(s_sq2, r + 1)
                for b in range(B):
                    ins = over_features(2 + b, sq2, b)
                ins.then_inc(s_ss2, 1)

            pe.wait_ge(s_h0, 4)
            for b in range(B):
                over_features(b, h0, b).then_inc(s_sum, 1)
            squares(0)

            def spread_b(st, n):
                c = st[1] % 2
                if n >= 2 or known(st, 1):
                    pe.wait_ge(s_bmul, cnt(N, st, 0, n - 1))
                if n == 0:
                    pe.wait_ge(s_lo, cnt(1, st, 1))
                M(ps[:, BB + n % 2, 0:T], sel[:, n, :], bcs[c][:, :], start=True, stop=True).then_inc(s_bb, 1)

            def phase_a(st, items):
                off = st[1]
                c = off % 2
                p = (off // 2) % 2
                po = ((off - 2) // 2) % 2
                for it in items:
                    if it == "outp" and known(st, 2):
                        pe.wait_ge(s_gate, cnt(1, st, -1))
                        pe.wait_ge(s_ow[po], cnt4(16, st, off - 2))
                        if isinstance(st[0], int):
                            pe.wait_ge(s_cc, N * min(st[0] + off, HS))
                        else:
                            pe.wait_ge(s_cc, cnt(N, st, 0))
                        for k in range(HK):
                            for j in range(IK):
                                ins = M(ps[0:HP, BA + k, 0:T], outw[po][:, j, k * HP:(k + 1) * HP], gt[:, j, :],
                                        start=(j == 0), stop=(j == IK - 1))
                            ins.then_inc(s_outp, 1)
                    if it == "ss":
                        pe.wait_ge(s_sq, cnt(1, st, 1))
                        if known(st, 1):
                            pe.wait_ge(s_cc, cnt(N, st, 0))
                        for k in range(HK):
                            ins = M(ps[0:HP, BA, 0:T], ones[0:HP, 0:HP], sq[:, k, :], start=(k == 0), stop=(k == HK - 1))
                        ins.then_inc(s_ss, 1)
                    if it[:3] == "inp":
                        m = int(it[3:])
                        if m == 0:
                            pe.wait_ge(s_xn, cnt(1, st, 1))
                            pe.wait_ge(s_w[p], cnt4(16 * NW, st, off))
                        if m >= 2:
                            pe.wait_ge(s_evac, cnt(2 * IK, st, 0, m - 1))
                        for k in range(HK):
                            ins = M(ps[:, BA + (m + 1) % 2, 0:T], inw[p][:, k, m * 128:(m + 1) * 128], xn[:, k, :],
                                    start=(k == 0), stop=(k == HK - 1))
                        ins.then_inc(s_inp, 1)
                    if it == "xproj":
                        pe.wait_ge(s_silu, cnt(1, st, 1))
                        if known(st, 0) and off < 2:
                            pe.wait_ge(s_cself, 6)
                        for k in range(IK):
                            ins = M(ps[0:96, BA + 1, 0:T], xpw[p][:, k, :], uz[c][:, k, :],
                                    start=(k == 0), stop=(k == IK - 1))
                        ins.then_inc(s_xproj, 1)
                    if it == "dtp":
                        pe.wait_ge(s_dtr, cnt(1, st, 1))
                        for m in range(IK):
                            if m == 1:
                                pe.wait_ge(s_r1, cnt(1, st, 1))
                            if m == 2:
                                pe.wait_ge(s_xpre, cnt(IK, st, 0, 1))
                            M(ps[:, BA + m % 2, 0:T], dtw[p][:, m * 128:(m + 1) * 128], dtr[:, :],
                              start=True, stop=True).then_inc(s_dtp, 1)
                    if it[:2] == "cb":
                        n = int(it[2:])
                        if n == 0:
                            pe.wait_ge(s_lo, cnt(1, st, 1))
                            pe.wait_ge(s_xpre, cnt(IK, st, 1))
                        if n >= 2:
                            pe.wait_ge(s_cc, cnt(N, st, 0, n - 1))
                        M(ps[:, BA + n % 2, 0:T], sel[:, N + n, :], bcs[c][:, :], start=True, stop=True)\
                            .then_inc(s_cb, 1)

            def sum_states(st, n):
                c = st[1] % 2
                parts = ((BY, 0, 512), (BY + 1, 512, W3T))
                if n == 0:
                    if known(st, 1):
                        pe.wait_ge(s_gate, cnt(1, st, 0))
                    pe.wait_ge(s_ud, cnt(IK, st, 1))
                    for bank, a, z in parts:
                        M(ps[:, bank, 0:z - a], ident[:, :], uD[c][:, a:z], start=True, stop=False)
                pe.wait_ge(s_cmul, cnt(N, st, 0, n + 1))
                for bank, a, z in parts:
                    ins = M(ps[:, bank, 0:z - a], ident[:, :], hc[:, n % RING, a:z], start=False, stop=(n == N - 1))
                ins.then_inc(s_ys, 1)

            def half_step(st, off):
                nxt = (st[0], off + 1)
                last = is_last(st)
                for n in range(N):
                    if n + 1 < N and n >= 1:
                        spread_b(st, n + 1)
                    if n >= 2:
                        sum_states(st, n - 2)
                    phase_a(nxt, [x for x in PE_A.get(n, ()) if not last or x == "outp"])
                if not last:
                    for n in range(2):
                        spread_b(nxt, n)
                for n in range(N - 2, N):
                    sum_states(st, n)

            pe.wait_ge(s_const, 4)
            phase_a((0, 0), sum(PE_A.values(), []))
            for n in range(2):
                spread_b((0, 0), n)
            steps_of(pe, half_step)
            phase_a((HS - 4, 5), ["outp"])

            squares(1)
            pe.wait_ge(s_h1, B * HK + 1)
            for b in range(B):
                over_features(b, h0, b).then_inc(s_sum, 1)
            squares(2)
            pe.wait_ge(s_lno, 4)
            pe.wait_ge(s_fw, 48)
            for j in range(5):
                n = min(128, B * T - 128 * j)
                o = ps[0:n, 4, j * NE:(j + 1) * NE]
                for k in range(HK):
                    M(o, xcf[:, k, 128 * j:128 * j + n], wg[:, k, :], start=(k == 0), stop=False)
                ins = M(o, ones[0:1, 0:n], bgr[:, :], start=False, stop=True)
            ins.then_inc(s_gatem, 1)
            pe.wait_ge(s_disp, 1)
            for j in range(5):
                n = min(128, B * T - 128 * j)
                ins = M(flat[0:NE, 2 * 512 + 128 * j:2 * 512 + 128 * j + n], disp[0:n, j, :], identb[0:n, 0:n],
                        start=True, stop=True)
            ins.then_inc(s_dispT, 1)
            pe.wait_ge(s_dispc, 1)
            for e in range(NE):
                if e >= 2:
                    pe.wait_ge(s_maskc, e - 1)
                for b in range(B):
                    ins = M(ps[0:HP, 2 * (e % 2) + b, 0:T], sel[0:NE, e, 0:HP], dispT[:, b * T:(b + 1) * T],
                            start=True, stop=True)
                ins.then_inc(s_mask, 1)

            def down(e, p, j):
                n = FS[j // B]
                pe.wait_ge(s_fmul, e * (B * FK) + (B * FK * p + j + 1))
                for k in range(HK):
                    ins = M(ps[0:HP, 4 + 2 * k + j % B, 0:T], e3[p][0:n, j // B, k * HP:(k + 1) * HP],
                            hf[0:n, j % HR, :],
                            start=(j < B and not known_expert(e, p)), stop=False)
                ins.then_inc(s_down, 1)

            def expert(e, p):
                pe.wait_ge(s_e[p], e * 32 + 64)
                pe.wait_ge(s_xmask, e + (p + 1))
                if not known_expert(e, p):
                    pe.wait_ge(s_maskc, NE)
                for j in range(B * FK):
                    ft, b = divmod(j, B)
                    n = FS[ft]
                    if known_expert(e, p) or j >= 2:
                        pe.wait_ge(s_fmul, e * (B * FK) + (B * FK * p + j - 1))
                    q = 2 * (j % 2)
                    for k in range(HK):
                        M(ps[0:n, q, 0:T], e1[p][:, k, 128 * ft:128 * ft + n], xcf[:, k, b * T:(b + 1) * T],
                          start=(k == 0), stop=(k == HK - 1))
                    for k in range(HK):
                        ins = M(ps[0:n, q + 1, 0:T], e2[p][:, k, 128 * ft:128 * ft + n],
                                xm[p][:, k, b * T:(b + 1) * T], start=(k == 0), stop=(k == HK - 1))
                    ins.then_inc(s_up, 1)
                    if j >= 1:
                        down(e, p, j - 1)
                down(e, p, B * FK - 1)

            experts_of(pe, expert)
            for k in range(HK):
                for b in range(B):
                    ins = M(ps[0:HP, 4 + 2 * k + b, 0:T], ident[0:HP, 0:HP], h0[:, k, b, :], start=False, stop=True)
            ins.then_inc(s_resid2, 1)
            pe.wait_ge(s_outT, HK)
            for b in range(B):
                for k, (t0, n) in enumerate(((0, 128), (128, 128), (256, 1))):
                    j = 3 * b + k
                    if j >= 4:
                        pe.wait_ge(s_outs, j - 3)
                    for q in range(HK):
                        ins = pe.transpose(ps[0:n, j % 4, q * HP:(q + 1) * HP], outT[:, q, b, t0:t0 + n],
                                           ident[0:HP, 0:HP])
                    ins.then_inc(s_tr, 1)


def kernel(**inputs):
    import numpy as _np
    import concourse.bacc as _bacc
    from concourse import mybir as _mybir
    from concourse.bass_utils import run_bass_kernel_spmd as _run

    v = {n: _np.asarray(a) for n, a in inputs.items()}
    x = v["x"]

    def patches(p):
        h = x.shape[2] // p
        return x.reshape(2, 3, h, p, h, p).transpose(2, 4, 0, 3, 5, 1).reshape(h * h, -1)

    def by_patch(w, p):
        return w.reshape(EMB, GP, 3 * p * p).transpose(2, 1, 0)

    def halves(w):
        return _np.moveaxis(w.reshape(*w.shape[:-1], HK, HP), -1, -2)

    def interpolation(length):
        m = _np.zeros((length, 256), _np.float32)
        pos = _np.clip((_np.arange(256) + 0.5) * (length / 256) - 0.5, 0, length - 1)
        lo = _np.floor(pos).astype(int)
        for t in range(256):
            m[lo[t], t] += 1 - (pos[t] - lo[t])
            m[min(lo[t] + 1, length - 1), t] += pos[t] - lo[t]
        return m

    a, t = "L0_attn_", "L0_tok_"
    prm = _np.concatenate([v[a + "conv_w"][:, :, 0, :]] + [v[a + n][:, :, None] for n in ("conv_b", "dt_proj_b", "D")]
                          + [v[a + "A_log"]], axis=2)
    lay = dict(
        P0=patches(1), P1=patches(2), P2=patches(4), idx0=v[t + "idx0"].reshape(2, 128, GP).transpose(1, 0, 2),
        idx1=v[t + "idx1"].reshape(8, 128).T, idx2=v[t + "idx2"].reshape(2, 128).T,
        W0T=v[t + "W0"].T, W1G=by_patch(v[t + "W1"], 2), W2G=by_patch(v[t + "W2"], 4),
        b0=v[t + "b0"][:, None], b1=v[t + "b1"], b2=v[t + "b2"], WfT=v[t + "Wf"].T, bf=halves(v[t + "bf"]),
        M1=interpolation(64), M2=interpolation(16), cls=halves(v["cls_tok"][0, 0]),
        in_wT=v[a + "in_proj_w"].transpose(0, 2, 1), x_wT=v[a + "x_proj_w"].transpose(0, 2, 1),
        dt_wT=v[a + "dt_proj_w"].transpose(0, 2, 1), out_wT=v[a + "out_proj_w"].transpose(0, 2, 1),
        prm_d=prm, norm_w=halves(v[a + "norm_w"]), final_w=halves(v[a + "final_norm_w"]),
        WgT=v["L0_ffn_Wg"].T, bg=v["L0_ffn_bg"], E1=v["L0_ffn_W1"].transpose(0, 2, 1),
        E2=v["L0_ffn_W2"].transpose(0, 2, 1), E3=v["L0_ffn_W3"].transpose(0, 2, 1))
    nc = _bacc.Bacc("TRN2", target_bir_lowering=False, num_devices=1)
    arrays, args = {}, {}
    for name, arr in lay.items():
        arr = _np.ascontiguousarray(arr)
        arrays[f"in_{name}"] = arr
        args[name] = nc.dram_tensor(f"in_{name}", arr.shape, _mybir.dt.from_np(arr.dtype), kind="ExternalInput").ap()
    out = nc.dram_tensor("out_h", (B, T, H), F32, kind="ExternalOutput").ap()
    mamba_vit(nc, out=out, **args)
    return _run(nc, [arrays], core_ids=[0]).results[0]["out_h"]
```

```python
from contextlib import ExitStack

import concourse.bass as bass
from concourse import mybir

ALU = mybir.AluOpType
ACT = mybir.ActivationFunctionType
F32 = mybir.dt.float32
BF16 = mybir.dt.bfloat16
AX = mybir.AxisListType

B = 2
T = 257
TP = T - 1
H = 192
HP = 96
HK = H // HP
I = 384
IK = I // 128
N = 16
R = 48
KC = 4
NL = 16
EPS = 1e-5
NE = 8
F = 469
FK = (F + 127) // 128
FS = [min(128, F - 128 * k) for k in range(FK)]
GP = 16
EMB = 64
W3T = IK * T
NPRM = KC + 3 + N
HR = 4
LN_EXP = "natural_log_exp_and_others"
RING = 4
NW = 6
HS = B * NL
BD, BB, BY, BA = 0, 2, 4, 6

DVE_ORDER = """gate bm0 pm0 sc0 sa0 resid0 bm1 pm1 resid1 sc1 sa1 bm2 pm2 sc2 sa2 bm3 newton pm3 xn sc3 sa3 bm4
    pm4 sc4 sa4 bm5 pm5 sc5 sa5 bm6 conv0 conv1 pm6 conv2 sc6 sa6 bm7 pm7 sc7 sa7 bm8 pm8 sc8 sa8 bm9 pm9 r1 sc9
    sa9 bm10 pm10 lo sc10 sa10 bm11 pm11 sc11 sa11 bm12 pm12 sc12 sa12 bm13 pm13 sc13 sa13 bm14 pm14 sc14 sa14
    bm15 pm15 sc15 sa15 nr m dt dtu""".split()
ACT_ORDER = """da0 da1 da2 sq0 sq1 rstd da3 da4 da5 ev0 diag da6 negA ev1 ev2 da7 ev3 da8 ev4 da9 ev5 siluU
    siluZ dtr hi da10 xa0 mid xa1 da11 xa2 da12 cc0 cc1 da13 da14 cc2 cc3 ex cc4 cc5 da15 cc6 cc7 wsum cc8 cc9
    lnx cc10 cc11 cc12 cc13 cc14 cc15""".split()
PE_ORDER = """outp0 outp1 ss0 bb2 bb3 ss1 ys0 bb4 ys1 bb5 inp0 inp1 ys2 inp2 bb6 ys3 inp3 inp4 bb7 inp5 bb8 ys4
    ys5 bb9 xproj ys6 dtp0 bb10 dtp1 ys7 bb11 dtp2 bb12 cb0 cb1 ys8 cb2 bb13 cb3 ys9 ys10 bb14 cb4 cb5 bb15 ys11
    next0 cb6 cb7 ys12 cb8 cb9 ys13 cb10 cb11 ys14 cb12 cb13 ys15 cb14 next1 cb15""".split()


def mamba_vit(nc, P0, P1, P2, idx0, idx1, idx2, W0T, W1G, W2G, b0, b1, b2, WfT, bf, M1, M2, cls,
              in_wT, x_wT, dt_wT, out_wT, prm_d, norm_w, final_w, WgT, bg, E1, E2, E3, out):
    ctx = ExitStack()
    with ctx:
        def sb(name, shape, dt=F32):
            return ctx.enter_context(nc.sbuf_tensor(name, shape, dt))

        def sem(name):
            return ctx.enter_context(nc.semaphore(name))

        ps = ctx.enter_context(nc.psum_tensor("ps", [128, 8, 512], F32))
        flat = ps[:, :, :].rearrange("p b n -> p (b n)")

        ident = sb("ident", [128, 128])
        ones = sb("ones", [128, 128])
        sel = sb("sel", [96, 2 * N, 128], BF16)
        iota8 = sb("iota8", [128, NE])
        i0 = sb("i0", [128, 2, GP], mybir.dt.int32)
        i1 = sb("i1", [128, 8], mybir.dt.int32)
        i2 = sb("i2", [128, 2], mybir.dt.int32)
        G0 = sb("G0", [128, 2, GP, 6])
        G0b = sb("G0b", [128, 2, B, GP * 3])
        G1 = sb("G1", [128, 8, 24])
        G2 = sb("G2", [128, 2, 96])
        w0 = sb("w0", [48, EMB])
        b0c = sb("b0c", [EMB, 1])
        b1r = sb("b1r", [1, EMB])
        b2r = sb("b2r", [1, EMB])
        wf = sb("wf", [EMB, 3, H])
        bfc = sb("bfc", [HP, HK])
        tok1 = sb("tok1", [64, B, EMB])
        tok2 = sb("tok2", [16, B, EMB])
        h0 = sb("h0", [HP, HK, B, T])
        clsb = sb("clsb", [HP, HK])
        xs = [sb(f"xs{c}", [HP, HK, T]) for c in range(B)]
        sq = sb("sq", [HP, HK, T])
        lnv = sb("lnv", [HP, T])
        var = sb("var", [HP, T])
        root = sb("root", [HP, T])
        rootsq = sb("rootsq", [HP, T])
        rstd = sb("rstd", [HP, T])
        xn = sb("xn", [HP, HK, T])
        fw = sb("fw", [HP, HK])
        inw = [sb(f"inw{p}", [HP, HK, 2 * I]) for p in range(2)]
        xpw = [sb(f"xpw{p}", [128, IK, 96]) for p in range(2)]
        dtw = [sb(f"dtw{p}", [R, I]) for p in range(2)]
        outw = [sb(f"outw{p}", [128, IK, H]) for p in range(2)]
        prm = [sb(f"prm{p}", [128, IK, NPRM]) for p in range(2)]
        nw = [sb(f"nw{p}", [HP, HK]) for p in range(2)]
        expA = [sb(f"expA{p}", [128, IK, N]) for p in range(2)]
        diagD = [sb(f"diagD{p}", [128, IK, 128]) for p in range(2)]
        negA = [sb(f"negA{p}", [128, IK, N]) for p in range(2)]
        uraw = sb("uraw", [128, IK, KC - 1 + T])
        uz = [sb(f"uz{c}", [128, 2 * IK, T]) for c in range(B)]
        dtr = sb("dtr", [R, T])
        bcs = [sb(f"bcs{c}", [96, T], BF16) for c in range(B)]
        bcr = sb("bcr", [64, T])
        xpre = sb("xpre", [128, W3T])
        absx = sb("absx", [128, W3T])
        ex = sb("ex", [128, W3T])
        w1p = sb("w1p", [128, W3T])
        ln1 = sb("ln1", [128, 1])
        lnx = sb("lnx", [128, W3T])
        dt = [sb(f"dt{c}", [128, IK, T]) for c in range(B)]
        dtu = [sb(f"dtu{c}", [128, IK, T]) for c in range(B)]
        cbc = [sb(f"cbc{c}", [128, N, T]) for c in range(B)]
        dA = sb("dA", [128, RING, IK, T])
        eps = sb("eps", [128, 1])
        hr = sb("hr", [128, RING, W3T])
        hc = sb("hc", [128, RING, W3T])
        gt = sb("gt", [128, IK, T])
        wg = sb("wg", [HP, HK, NE])
        bgr = sb("bgr", [1, NE])
        gate = sb("gate", [128, 5, NE])
        mx = sb("mx", [128, 5])
        eq = sb("eq", [128, 5, NE])
        cand = sb("cand", [128, 5, NE])
        first = sb("first", [128, 5])
        oneh = sb("oneh", [128, 5, NE])
        dif = sb("dif", [128, 5])
        prob = sb("prob", [128, 5])
        rden = sb("rden", [128, 5])
        pn = sb("pn", [128, 5])
        disp = sb("disp", [128, 5, NE], BF16)
        e1 = [sb(f"e1{p}", [HP, HK, F]) for p in range(2)]
        e2 = [sb(f"e2{p}", [HP, HK, F]) for p in range(2)]
        e3 = [sb(f"e3{p}", [128, FK, H]) for p in range(2)]
        dispT = sb("dispT", [NE, B * T], BF16)
        identb = sb("identb", [128, 128], BF16)

        def inside(buf, at, parts, **dims):
            names, n = " ".join(dims), 1
            for d in dims.values():
                n *= d
            v = buf[0:parts, at:at + n]
            sizes = dict(list(dims.items())[1:])
            return v.rearrange(f"p ({names}) -> p {names}", **sizes) if len(dims) > 1 else v

        cb0, cb1 = (cbc[c][:, :, :].rearrange("p n t -> p (n t)") for c in range(B))
        hcf = hc[:, :, :].rearrange("p r n -> p (r n)")
        hrf = hr[:, :, :].rearrange("p r n -> p (r n)")
        GT0 = inside(cb0, 0, 48, n=512)
        GT1 = inside(cb0, 512, 12, n=2048)
        GT2 = inside(cb0, 2560, 48, n=512)
        w1 = inside(cb0, 3072, 12, g=GP, e=EMB)
        w2 = inside(cb1, 0, 48, g=GP, e=EMB)
        cat = inside(cb1, 1024, EMB, l=3, n=512)
        m1 = inside(cb1, 2560, 64, n=256)
        m2 = inside(cb1, 2816, 16, n=256)
        xc = inside(hcf, 0, HP, k=HK, b=B, t=T)
        sq2 = inside(hcf, HK * B * T, HP, k=HK, b=B, t=T)
        lnv2 = inside(hcf, 2 * HK * B * T, HP, b=B, t=T)
        var2 = inside(hrf, 0, HP, b=B, t=T)
        root2 = inside(hrf, B * T, HP, b=B, t=T)
        rstd2 = inside(hcf, 2 * HK * B * T + B * T, HP, b=B, t=T)
        maskb = inside(cb0, 0, HP, e=NE, n=B * T)
        xm = [inside(cb1, p * HK * B * T, HP, k=HK, n=B * T) for p in range(2)]
        uzf = uz[0][:, :, :].rearrange("p k t -> p (k t)")
        hf = inside(uzf, 0, 128, r=HR, t=T)
        sg = inside(uzf, HR * T, 128, r=2, t=T)
        outT = inside(cb1, 2 * HK * B * T, HP, k=HK, b=B, t=T)
        outs = inside(hrf, 2 * B * T, 128, j=B * 3, h=H)

        block = ctx.enter_context(nc.Block())

        s_idx, s_tokw, s_cls = sem("s_idx"), sem("s_tokw"), sem("s_cls")
        s_zero, s_const = sem("s_zero"), sem("s_const")
        s_gather12, s_gather0 = sem("s_gather12"), sem("s_gather0")
        s_gt, s_gtc, s_tokm, s_tokc, s_int, s_intc, s_fuse, s_h0 = (
            sem(n) for n in ("s_gt", "s_gtc", "s_tokm", "s_tokc", "s_int", "s_intc", "s_fuse", "s_h0"))
        s_sum, s_xc, s_sq2, s_ss2, s_ln2, s_rs2, s_lno = (
            sem(n) for n in ("s_sum", "s_xc", "s_sq2", "s_ss2", "s_ln2", "s_rs2", "s_lno"))
        s_w = [sem(f"s_w{p}") for p in range(2)]
        s_ow = [sem(f"s_ow{p}") for p in range(2)]
        (s_gate, s_outp, s_resid, s_sq, s_ss, s_ln, s_rstd, s_xn, s_inp, s_evac, s_conv, s_silu, s_diag,
         s_xproj, s_dtr, s_hi, s_r1, s_mid, s_lo, s_dtp, s_xpre, s_ex, s_w1p, s_lnx, s_ln1, s_nr, s_m,
         s_dt, s_dtu, s_cb, s_cc, s_negA, s_cself, s_ctap, s_rt, s_gate0, s_root, s_rootsq, s_newton,
         s_root2, s_rsq2, s_g0b, s_resid2, s_disp, s_dispT, s_dispc, s_mask, s_maskc) = (
            sem(n) for n in (
                "s_gate s_outp s_resid s_sq s_ss s_ln s_rstd s_xn s_inp s_evac s_conv s_silu s_diag "
                "s_xproj s_dtr s_hi s_r1 s_mid s_lo s_dtp s_xpre s_ex s_w1p s_lnx s_ln1 s_nr s_m "
                "s_dt s_dtu s_cb s_cc s_negA s_cself s_ctap s_rt s_gate0 s_root s_rootsq s_newton "
                "s_root2 s_rsq2 s_g0b s_resid2 s_disp s_dispT s_dispc s_mask s_maskc").split())
        s_bb, s_dA, s_bmul0, s_bmul, s_scan0, s_scan, s_cmul, s_ys = (
            sem(n) for n in ("s_bb", "s_dA", "s_bmul0", "s_bmul", "s_scan0", "s_scan", "s_cmul", "s_ys"))
        s_h1, s_gatem, s_route, s_prob, s_fw, s_xmask, s_up, s_act, s_fmul, s_down = (
            sem(n) for n in ("s_h1", "s_gatem", "s_route", "s_prob", "s_fw", "s_xmask", "s_up",
                             "s_act", "s_fmul", "s_down"))
        s_e = [sem(f"s_e{p}") for p in range(2)]
        s_outT, s_tr, s_outs, s_out = sem("s_outT"), sem("s_tr"), sem("s_outs"), sem("s_out")

        def cnt(k, st, steps, c=0):
            b4, off = st
            return b4 * k + (k * (off + steps) + c)

        def cnt4(k, st, off):
            b4, _ = st
            return b4 * (k // 4) + k * (off // 4 + 1)

        def known(st, n):
            return not isinstance(st[0], int) or st[0] + st[1] >= n

        def is_last(st):
            return isinstance(st[0], int) and st[0] + st[1] == HS - 1

        def steps_of(eng, half_step):
            half_step((0, 0), 0)
            with eng.Fori(0, HS - 4, 4) as b4:
                for off in range(1, 5):
                    half_step((b4, off), off)
            for off in range(1, 4):
                half_step((HS - 4, off), off)

        def known_expert(e, p):
            return not isinstance(e, int) or e + p >= 1

        def experts_of(eng, expert):
            for p in range(2):
                expert(0, p)
            with eng.Fori(1, NE // 2) as pair:
                for p in range(2):
                    expert(pair * 2, p)

        xcf = xc[:, :, :, :].rearrange("p k b t -> p k (b t)")

        @block.sync
        def _(sp):
            sp.dma_start(i0[:, :, :], idx0).then_inc(s_idx, 16)
            sp.dma_start(i1[:, :], idx1).then_inc(s_idx, 16)
            sp.dma_start(i2[:, :], idx2).then_inc(s_idx, 16)
            for dst, src in ((w0[:, :], W0T), (w1[:, :, :], W1G), (w2[:, :, :], W2G),
                             (b0c[:, :], b0),
                             (b1r[:, :], b1.rearrange("(a n) -> a n", a=1)),
                             (b2r[:, :], b2.rearrange("(a n) -> a n", a=1)),
                             (wf[:, :, :], WfT.rearrange("(l p) o -> p l o", p=EMB)),
                             (bfc[:, :], bf),
                             (m1[:, :], M1), (m2[:, :], M2)):
                sp.dma_start(dst, src).then_inc(s_tokw, 16)
            sp.dma_start(clsb[:, :], cls).then_inc(s_cls, 16)

            def load_layer(lyr, p):
                sp.dma_start(inw[p][:, :, :], in_wT[lyr].rearrange("(k p) c -> p k c", p=HP)).then_inc(s_w[p], 16)
                x_w = x_wT[lyr].rearrange("(k p) c -> p k c", p=128)
                sp.dma_start(xpw[p][:, :, 0:R], x_w[:, :, 0:R]).then_inc(s_w[p], 16)
                sp.dma_start(xpw[p][:, :, 64:96], x_w[:, :, R:R + 2 * N]).then_inc(s_w[p], 16)
                sp.dma_start(dtw[p][:, :], dt_wT[lyr]).then_inc(s_w[p], 16)
                sp.dma_start(prm[p][:, :, :], prm_d[lyr].rearrange("(k p) c -> p k c", p=128)).then_inc(s_w[p], 16)
                sp.dma_start(nw[p][:, :], norm_w[lyr]).then_inc(s_w[p], 16)

            def load_out(lyr, p):
                sp.dma_start(outw[p][:, :, :], out_wT[lyr].rearrange("(k p) c -> p k c", p=128)).then_inc(s_ow[p], 16)

            for p in range(2):
                load_layer(p, p)
                load_out(p, p)
            for dst, src in ((fw[:, :], final_w),
                             (wg[:, :, :], WgT.rearrange("(k p) e -> p k e", p=HP)),
                             (bgr[:, :], bg.rearrange("(a n) -> a n", a=1))):
                sp.dma_start(dst, src).then_inc(s_fw, 16)

            def load_expert(e, p):
                sp.dma_start(e1[p][:, :, :], E1[e].rearrange("(k p) f -> p k f", p=HP)).then_inc(s_e[p], 16)
                sp.dma_start(e2[p][:, :, :], E2[e].rearrange("(k p) f -> p k f", p=HP)).then_inc(s_e[p], 16)
                sp.dma_start(e3[p][:, 0:FK - 1, :], E3[e, 0:128 * (FK - 1)].rearrange("(k p) d -> p k d", p=128))\
                  .then_inc(s_e[p], 16)
                sp.dma_start(e3[p][0:FS[-1], FK - 1, :], E3[e, 128 * (FK - 1):F]).then_inc(s_e[p], 16)

            for p in range(2):
                load_expert(p, p)
            with sp.Fori(0, NL // 2 - 1) as pair:
                l2 = pair * 2
                for p in range(2):
                    sp.wait_ge(s_xpre, l2 * (2 * IK) + 2 * IK * (p + 1))
                    load_layer(l2 + (p + 2), p)
                    sp.wait_ge(s_outp, l2 * (2 * HK) + 2 * HK * (p + 1))
                    load_out(l2 + (p + 2), p)
            with sp.Fori(0, NE // 2 - 1) as pair:
                e2l = pair * 2
                for p in range(2):
                    sp.wait_ge(s_down, e2l * (2 * FK) + 2 * FK * (p + 1))
                    load_expert(e2l + (p + 2), p)
            for b in range(B):
                for k, (t0, n) in enumerate(((0, 128), (128, 128), (256, 1))):
                    sp.wait_ge(s_outs, 3 * b + k + 1)
                    sp.dma_start(out[b, t0:t0 + n, :], outs[0:n, 3 * b + k, :]).then_inc(s_out, 16)
            sp.wait_ge(s_out, 16 * B * 3)

        @block.gpsimd
        def _(pool):
            pool.memset(ident[:, :], 0.0).then_inc(s_zero, 1)
            pool.wait_ge(s_zero, 1)
            pool.affine_select(out=ident[:, :], in_=ident[:, :], compare_op=ALU.not_equal, fill=1.0, base=0,
                               pattern=[[-1, 128]], channel_multiplier=1).then_inc(s_const, 1)
            pool.wait_ge(s_idx, 48)
            pool.wait_ge(s_const, 1)
            for q in range(8):
                pool.indirect_dma_start(out=G1[:, q, :], out_offset=None, in_=P1[:, :],
                                        in_offset=bass.IndirectOffsetOnAxis(ap=i1[:, q:q + 1], axis=0))\
                    .then_inc(s_gather12, 16)
            for q in range(2):
                pool.indirect_dma_start(out=G2[:, q, :], out_offset=None, in_=P2[:, :],
                                        in_offset=bass.IndirectOffsetOnAxis(ap=i2[:, q:q + 1], axis=0))\
                    .then_inc(s_gather12, 16)
            for k in range(2):
                for g in range(GP):
                    pool.indirect_dma_start(out=G0[:, k, g, :], out_offset=None, in_=P0[:, :],
                                            in_offset=bass.IndirectOffsetOnAxis(ap=i0[:, k, g:g + 1], axis=0))\
                        .then_inc(s_gather0, 16)
            pool.wait_ge(s_gather12, 16 * 10)
            pool.wait_ge(s_gather0, 16 * 2 * GP)
            pool.memset(sel[:, :, :], 0.0).then_inc(s_zero, 1)
            pool.wait_ge(s_zero, 2)
            for j in range(3):
                blk = sel[32 * j:32 * j + 32, :, :]
                pool.affine_select(out=blk, in_=blk, compare_op=ALU.not_equal, fill=1.0, base=0,
                                   pattern=[[-1, 2 * N], [0, 128]], channel_multiplier=1).then_inc(s_const, 1)
                pool.wait_ge(s_const, 2 + j)
            pool.iota(iota8[:, :], pattern=[[1, NE]], base=-NE, channel_multiplier=0,
                      allow_small_or_imprecise_dtypes=True).then_inc(s_const, 1)

            def half_step(st, off):
                c = off % 2
                for n in range(N):
                    pool.wait_ge(s_scan, cnt(N, st, 0, n + 1))
                    pool.wait_ge(s_cc, cnt(N, st, 0, n + 1))
                    if n >= RING or known(st, 1):
                        pool.wait_ge(s_ys, cnt(N, st, 0, n - RING + 1))
                    pool.tensor_tensor(hc[:, n % RING, :].rearrange("p (k t) -> p k t", k=IK),
                                       hr[:, n % RING, :].rearrange("p (k t) -> p k t", k=IK),
                                       cbc[c][:, n:n + 1, :].broadcast_to([128, IK, T]), ALU.mult)\
                        .then_inc(s_cmul, 1)

            steps_of(pool, half_step)

            def masked(e, p):
                pool.wait_ge(s_maskc, e + (p + 1))
                for k in range(HK):
                    ins = pool.tensor_tensor(xm[p][:, k, :], xcf[:, k, :], maskb[:, bass.ds(e + p, 1), :]
                                             .rearrange("p a t -> p (a t)"), ALU.mult)
                ins.then_inc(s_xmask, 1)

            pool.wait_ge(s_lno, 4)
            for p in range(2):
                masked(0, p)
            with pool.Fori(1, NE // 2) as pair:
                e = pair * 2
                for p in range(2):
                    pool.wait_ge(s_up, e * (2 * FK) + 2 * FK * (p - 1))
                    masked(e, p)

        @block.scalar
        def _(act):
            A = act.activation
            act.wait_ge(s_gt, 1)
            A(GT2[:, :], ps[0:48, 5, :], ACT.Copy).then_inc(s_gtc, 1)
            act.wait_ge(s_tokm, 1)
            A(tok1[:, :, :], ps[0:64, 7, 0:128].rearrange("p (b e) -> p b e", b=B), ACT.Copy).then_inc(s_tokc, 1)
            A(tok2[:, :, :], ps[0:16, 7, 128:256].rearrange("p (b e) -> p b e", b=B), ACT.Copy).then_inc(s_tokc, 1)
            act.wait_ge(s_int, 1)
            A(cat[:, 1:3, :], ps[0:EMB, 0:2, :], ACT.Copy).then_inc(s_intc, 1)
            act.wait_ge(s_gt, 2)
            A(GT0[:, :], ps[0:48, 4, :], ACT.Copy).then_inc(s_gtc, 1)
            act.wait_ge(s_tokw, 160)
            act.wait_ge(s_tokm, 2)
            A(cat[:, 0, :], ps[0:EMB, 6, :], ACT.Identity, bias=b0c[:, :]).then_inc(s_tokc, 1)
            act.wait_ge(s_fuse, 1)
            for k in range(HK):
                A(h0[:, k, :, 1:T], ps[0:HP, 2 + k, :].rearrange("p (b t) -> p b t", b=B), ACT.Identity,
                  bias=bfc[:, k:k + 1]).then_inc(s_h0, 1)
            act.wait_ge(s_cls, 16)
            for b in range(B):
                A(h0[:, :, b, 0], clsb[:, :], ACT.Copy).then_inc(s_h0, 1)

            def layer_norm(r):
                act.wait_ge(s_xc, B * (r // 2 + 1))
                A(sq2[:, :, :, :].rearrange("p k b t -> p (k b t)"), xc[:, :, :, :].rearrange("p k b t -> p (k b t)"),
                  ACT.Square).then_inc(s_sq2, 1)
                inverse_root(r)

            def inverse_root(r):
                act.wait_ge(s_ss2, r + 1)
                A(var2[:, :, :], ps[0:HP, 2:4, 0:T], ACT.Identity, bias=eps[0:HP, :], scale=1.0 / H)
                A(lnv2[:, :, :], ps[0:HP, 2:4, 0:T], ACT.Ln, bias=eps[0:HP, :], scale=1.0 / H).then_inc(s_ln2, 1)
                act.wait_ge(s_ln2, r + 1)
                A(root2[:, :, :], lnv2[:, :, :], ACT.Exp, scale=-0.5).then_inc(s_root2, 1)
                act.wait_ge(s_root2, r + 1)
                A(lnv2[:, :, :], root2[:, :, :], ACT.Square).then_inc(s_rsq2, 1)

            act.preload_act_table_set(LN_EXP)
            act.wait_ge(s_cself, 4)
            layer_norm(0)

            def decays(st, n):
                c, p = st[1] % 2, (st[1] // 2) % 2
                if n == 0:
                    act.wait_ge(s_dt, cnt(1, st, 1))
                    act.wait_ge(s_negA, cnt(1, st, 1 + (st[1] + 1) % 2))
                if n >= RING or known(st, 1):
                    act.wait_ge(s_scan, cnt(N, st, 0, n - RING + 1))
                elif n == 0:
                    act.wait_ge(s_cself, 2)
                for k in range(IK):
                    ins = A(dA[:, n % RING, k, 1:T], dt[c][:, k, 1:T], ACT.Exp, scale=negA[p][:, k, n:n + 1])
                ins.then_inc(s_dA, 1)

            def phase_a(st, it):
                off = st[1]
                c, p = off % 2, (off // 2) % 2
                if it == "negA" and off % 2 == 0:
                    act.wait_ge(s_w[p], cnt4(16 * NW, st, off))
                    A(expA[p][:, :, :], prm[p][:, :, KC + 3:NPRM], ACT.Exp).then_inc(s_negA, 1)
                    act.wait_ge(s_negA, cnt(1, st, 1))
                    A(negA[p][:, :, :], expA[p][:, :, :], ACT.Copy, scale=-1.0).then_inc(s_negA, 1)
                if it == "diag" and off % 2 == 0:
                    act.wait_ge(s_const, 1)
                    act.wait_ge(s_w[p], cnt4(16 * NW, st, off))
                    for k in range(IK):
                        ins = A(diagD[p][:, k, :], ident[:, :], ACT.Copy, scale=prm[p][:, k, KC + 2:KC + 3])
                    ins.then_inc(s_diag, 2)
                if it[:2] == "sq":
                    k = int(it[2:])
                    if known(st, 2):
                        act.wait_ge(s_resid, cnt(HK, st, -2, k + 1))
                    else:
                        act.wait_ge(s_lno, 2)
                    A(sq[:, k, :], xs[c][:, k, :], ACT.Square).then_inc(s_sq, 1)
                if it == "rstd":
                    act.wait_ge(s_ss, cnt(1, st, 1))
                    A(lnv[:, :], ps[0:HP, BA, 0:T], ACT.Ln, bias=eps[0:HP, :], scale=1.0 / H).then_inc(s_ln, 1)
                    A(var[:, :], ps[0:HP, BA, 0:T], ACT.Identity, bias=eps[0:HP, :], scale=1.0 / H)
                    act.wait_ge(s_ln, cnt(1, st, 1))
                    A(root[:, :], lnv[:, :], ACT.Exp, scale=-0.5).then_inc(s_root, 1)
                    act.wait_ge(s_root, cnt(1, st, 1))
                    A(rootsq[:, :], root[:, :], ACT.Square).then_inc(s_rootsq, 1)
                if it[:2] == "ev":
                    m = int(it[2:])
                    act.wait_ge(s_inp, cnt(2 * IK, st, 0, m + 1))
                    src = ps[:, BA + (m + 1) % 2, 0:T]
                    if m < IK:
                        if known(st, 1):
                            act.wait_ge(s_conv, cnt(IK, st, 0))
                        A(uraw[:, m, KC - 1:], src, ACT.Copy)
                        A(uz[c][:, m, :], src, ACT.Identity, scale=prm[p][:, m, KC - 1:KC],
                          bias=prm[p][:, m, KC:KC + 1]).then_inc(s_evac, 1)
                    else:
                        A(uz[c][:, m, :], src, ACT.Copy).then_inc(s_evac, 1)
                if it == "siluU":
                    act.wait_ge(s_conv, cnt(IK, st, 1))
                    A(uz[c][:, 0:IK, :], uz[c][:, 0:IK, :], ACT.Silu).then_inc(s_silu, 1)
                if it == "siluZ":
                    act.wait_ge(s_evac, cnt(2 * IK, st, 1))
                    A(uz[c][:, IK:, :], uz[c][:, IK:, :], ACT.Silu).then_inc(s_silu, 1)
                    act.preload_act_table_set(LN_EXP)
                if it == "dtr":
                    act.wait_ge(s_xproj, cnt(1, st, 1))
                    A(dtr[:, :], ps[0:R, BA + 1, 0:T], ACT.Copy).then_inc(s_dtr, 1)
                if it == "hi":
                    A(bcs[c][0:32, :], ps[64:96, BA + 1, 0:T], ACT.Copy).then_inc(s_hi, 1)
                if it == "mid":
                    act.wait_ge(s_r1, cnt(1, st, 1))
                    A(bcs[c][32:64, :], bcr[32:64, :], ACT.Copy).then_inc(s_mid, 1)
                if it[:2] == "xa":
                    m = int(it[2:])
                    if m == 0 and known(st, 1):
                        act.wait_ge(s_dt, cnt(1, st, 0))
                    act.wait_ge(s_dtp, cnt(IK, st, 0, m + 1))
                    bias = prm[p][:, m, KC + 1:KC + 2]
                    A(absx[:, m * T:(m + 1) * T], ps[:, BA + m % 2, 0:T], ACT.Abs, bias=bias)
                    A(xpre[:, m * T:(m + 1) * T], ps[:, BA + m % 2, 0:T], ACT.Identity, bias=bias).then_inc(s_xpre, 1)
                if it == "ex":
                    act.wait_ge(s_xpre, cnt(IK, st, 1))
                    A(ex[:, :], absx[:, :], ACT.Exp, scale=-1.0).then_inc(s_ex, 1)
                if it == "wsum":
                    act.wait_ge(s_ex, cnt(1, st, 1))
                    A(w1p[:, :], ex[:, :], ACT.Identity, bias=ones[:, 0:1]).then_inc(s_w1p, 1)
                if it == "lnx":
                    act.wait_ge(s_ex, cnt(1, st, 1))
                    A(lnx[:, :], ex[:, :], ACT.Ln, bias=ones[:, 0:1]).then_inc(s_lnx, 1)
                if it[:2] == "cc":
                    n = int(it[2:])
                    act.wait_ge(s_cb, cnt(N, st, 0, n + 1))
                    A(cbc[c][:, n, :], ps[:, BA + n % 2, 0:T], ACT.Copy).then_inc(s_cc, 1)

            def half_step(st, off):
                nxt, last = (st[0], off + 1), is_last(st)
                for it in ACT_ORDER:
                    if it[:2] == "da":
                        decays(st, int(it[2:]))
                    elif not last:
                        phase_a(nxt, it)

            A(ln1[:, :], ones[:, 0:1], ACT.Ln).then_inc(s_ln1, 1)
            for it in ACT_ORDER:
                if it[:2] != "da":
                    phase_a((0, 0), it)
            steps_of(act, half_step)

            act.wait_ge(s_resid, HK * HS)
            for c in range(B):
                ins = A(sq2[:, :, c, :], xs[c][:, :, :], ACT.Square)
            ins.then_inc(s_sq2, 1)
            inverse_root(1)
            layer_norm(2)
            act.wait_ge(s_route, 2)
            A(prob[:, :], dif[:, :], ACT.Exp).then_inc(s_prob, 1)

            def expert(e, p):
                for j in range(B * FK):
                    n = FS[j // B]
                    act.wait_ge(s_up, e * (B * FK) + (B * FK * p + j + 1))
                    if known_expert(e, p) or j >= 2:
                        act.wait_ge(s_fmul, e * (B * FK) + (B * FK * p + j - 1))
                    A(sg[0:n, j % 2, :], ps[0:n, 2 * (j % 2), 0:T], ACT.Silu).then_inc(s_act, 1)

            experts_of(act, expert)
            act.wait_ge(s_resid2, 1)
            for k in range(HK):
                A(outT[:, k, :, :], ps[0:HP, 4 + 2 * k:6 + 2 * k, 0:T], ACT.Copy).then_inc(s_outT, 1)
            for b in range(B):
                for k, n in enumerate((128, 128, 1)):
                    j = 3 * b + k
                    act.wait_ge(s_tr, j + 1)
                    A(outs[0:n, j, :], ps[0:n, j % 4, 0:H], ACT.Copy).then_inc(s_outs, 1)

        @block.vector
        def _(dve):
            V = nc.vector
            V.memset(ones[:, :], 1.0).then_inc(s_cself, 1)
            V.memset(dA[:, :, :, 0:1], 0.0).then_inc(s_cself, 1)
            V.memset(uraw[:, :, 0:KC - 1], 0.0).then_inc(s_cself, 1)
            V.memset(eps[:, :], EPS).then_inc(s_cself, 1)
            for p in range(2):
                V.memset(xpw[p][:, :, R:64], 0.0).then_inc(s_cself, 1)
            dve.wait_ge(s_gt, 1)
            for b in range(B):
                V.tensor_copy(GT1[:, b * 1024:(b + 1) * 1024], flat[0:12, (1 + 2 * b) * 512:(3 + 2 * b) * 512])\
                    .then_inc(s_gtc, 1)
            dve.wait_ge(s_gather0, 16 * 2 * GP)
            for b in range(B):
                V.tensor_copy(G0b[:, :, b, :].rearrange("p k (g c) -> p k g c", c=3), G0[:, :, :, 3 * b:3 * b + 3])\
                    .then_inc(s_g0b, 1)

            def centre(r, src):
                for b in range(B):
                    dve.wait_ge(s_sum, B * r + b + 1)
                    for k in range(HK):
                        ins = V.scalar_tensor_tensor(out=xc[:, k, b, :], in0=ps[0:HP, b, 0:T], scalar=-1.0 / H,
                                                     in1=src[:, k, b, :], op0=ALU.mult, op1=ALU.add)
                    ins.then_inc(s_xc, 1)

            def newton2(r):
                dve.wait_ge(s_rsq2, r + 1)
                V.scalar_tensor_tensor(out=var2[:, :, :], in0=lnv2[:, :, :], scalar=-0.5, in1=var2[:, :, :],
                                       op0=ALU.mult, op1=ALU.mult).then_inc(s_rs2, 1)
                dve.wait_ge(s_rs2, 2 * r + 1)
                V.scalar_tensor_tensor(out=rstd2[:, :, :], in0=var2[:, :, :], scalar=1.5, in1=root2[:, :, :],
                                       op0=ALU.add, op1=ALU.mult).then_inc(s_rs2, 1)
                dve.wait_ge(s_rs2, 2 * r + 2)

            dve.wait_ge(s_h0, 4)
            centre(0, h0)
            newton2(0)
            dve.wait_ge(s_xc, 2)
            for c in range(B):
                V.tensor_tensor(xs[c][:, :, :], xc[:, :, c, :],
                                rstd2[:, c:c + 1, :].broadcast_to([HP, HK, T]), ALU.mult).then_inc(s_lno, 1)

            def phase_a(st, it):
                off = st[1]
                c, p = off % 2, (off // 2) % 2
                if it == "gate" and known(st, 2):
                    dve.wait_ge(s_ys, cnt(N, st, -1))
                    dve.wait_ge(s_silu, cnt(2, st, -1))
                    V.tensor_tensor(gt[:, :, :].rearrange("p k t -> p (k t)"), flat[:, BY * 512:BY * 512 + W3T],
                                    uz[c][:, IK:2 * IK, :].rearrange("p k t -> p (k t)"), ALU.mult)\
                        .then_inc(s_gate, 1)
                if it[:5] == "resid" and known(st, 2):
                    k = int(it[5:])
                    dve.wait_ge(s_outp, cnt(HK, st, -2, k + 1))
                    V.tensor_tensor(xs[c][:, k, :], ps[0:HP, BA + k, 0:T], xs[c][:, k, :], ALU.add)\
                        .then_inc(s_resid, 1)
                if it == "newton":
                    dve.wait_ge(s_rootsq, cnt(1, st, 1))
                    V.scalar_tensor_tensor(out=lnv[:, :], in0=rootsq[:, :], scalar=-0.5, in1=var[:, :],
                                           op0=ALU.mult, op1=ALU.mult).then_inc(s_newton, 1)
                    dve.wait_ge(s_newton, cnt(1, st, 1))
                    V.scalar_tensor_tensor(out=rstd[:, :], in0=lnv[:, :], scalar=1.5, in1=root[:, :],
                                           op0=ALU.add, op1=ALU.mult).then_inc(s_rstd, 1)
                if it == "xn":
                    dve.wait_ge(s_rstd, cnt(1, st, 1))
                    dve.wait_ge(s_w[p], cnt4(16 * NW, st, off))
                    if known(st, 1):
                        dve.wait_ge(s_inp, cnt(2 * IK, st, 0))
                    for k in range(HK):
                        ins = V.scalar_tensor_tensor(out=xn[:, k, :], in0=xs[c][:, k, :], scalar=nw[p][:, k:k + 1],
                                                     in1=rstd[:, :], op0=ALU.mult, op1=ALU.mult)
                    ins.then_inc(s_xn, 1)
                if it[:4] == "conv":
                    m = int(it[4:])
                    dve.wait_ge(s_evac, cnt(2 * IK, st, 0, m + 1))
                    for j in range(KC - 1):
                        if j:
                            dve.wait_ge(s_ctap, cnt(IK * (KC - 2), st, 0, m * (KC - 2) + j))
                        V.scalar_tensor_tensor(out=uz[c][:, m, :], in0=uraw[:, m, j:j + T],
                                               scalar=prm[p][:, m, j:j + 1], in1=uz[c][:, m, :],
                                               op0=ALU.mult, op1=ALU.add)\
                            .then_inc(s_conv if j == KC - 2 else s_ctap, 1)
                if it == "r1":
                    dve.wait_ge(s_hi, cnt(1, st, 1))
                    V.tensor_tensor(bcr[32:64, :], ps[64:96, BA + 1, 0:T], bcs[c][0:32, :], ALU.subtract)\
                        .then_inc(s_r1, 1)
                if it == "lo":
                    dve.wait_ge(s_mid, cnt(1, st, 1))
                    V.tensor_tensor(bcs[c][64:96, :], bcr[32:64, :], bcs[c][32:64, :], ALU.subtract)\
                        .then_inc(s_lo, 1)
                if it == "nr":
                    dve.wait_ge(s_w1p, cnt(1, st, 1))
                    V.scalar_tensor_tensor(out=w1p[:, :], in0=w1p[:, :], scalar=-1.0, in1=ex[:, :],
                                           op0=ALU.add, op1=ALU.subtract).then_inc(s_nr, 1)
                if it == "m":
                    dve.wait_ge(s_nr, cnt(1, st, 1))
                    V.scalar_tensor_tensor(out=xpre[:, :], in0=xpre[:, :], scalar=0.0, in1=w1p[:, :],
                                           op0=ALU.max, op1=ALU.subtract).then_inc(s_m, 1)
                if it == "dt":
                    dve.wait_ge(s_lnx, cnt(1, st, 1))
                    dve.wait_ge(s_m, cnt(1, st, 1))
                    dve.wait_ge(s_ln1, 1)
                    V.scalar_tensor_tensor(out=dt[c][:, :, :].rearrange("p k t -> p (k t)"), in0=lnx[:, :],
                                           scalar=ln1[:, :], in1=xpre[:, :], op0=ALU.subtract, op1=ALU.add)\
                        .then_inc(s_dt, 1)
                if it == "dtu":
                    dve.wait_ge(s_dt, cnt(1, st, 1))
                    dve.wait_ge(s_silu, cnt(2, st, 0, 1))
                    V.tensor_tensor(dtu[c][:, :, :], dt[c][:, :, :], uz[c][:, 0:IK, :], ALU.mult)\
                        .then_inc(s_dtu, 1)

            def half_step(st, off):
                c = off % 2
                nxt, last = (st[0], off + 1), is_last(st)
                parts = {"bm": (0, 2), "sc": (0, 2), "pm": (2, IK), "sa": (2, IK)}
                for it in DVE_ORDER:
                    if it[:2] in parts:
                        n = int(it[2:])
                        k0, k1 = parts[it[:2]]
                        dbu = flat[:, BD * 512 + k0 * T:BD * 512 + k1 * T]
                        product, scan = (s_bmul0, s_scan0) if k0 == 0 else (s_bmul, s_scan)
                    if it[:2] in ("pm", "bm"):
                        if n == 0:
                            dve.wait_ge(s_dtu, cnt(1, st, 1))
                        dve.wait_ge(s_bb, cnt(N, st, 0, n + 1))
                        if n or known(st, 1):
                            dve.wait_ge(scan, cnt(N, st, 0, n))
                        V.tensor_tensor(dbu.rearrange("p (k t) -> p k t", t=T), dtu[c][:, k0:k1, :],
                                        ps[:, BB + n % 2, 0:T].rearrange("p (a t) -> p a t", a=1)
                                        .broadcast_to([128, k1 - k0, T]), ALU.mult).then_inc(product, 1)
                    elif it[:2] in ("sa", "sc"):
                        dve.wait_ge(s_dA, cnt(N, st, 0, n + 1))
                        dve.wait_ge(product, cnt(N, st, 0, n + 1))
                        if n >= RING or known(st, 1):
                            dve.wait_ge(s_cmul, cnt(N, st, 0, n - RING + 1))
                        V.tensor_tensor_scan(hr[:, n % RING, k0 * T:k1 * T],
                                             dA[:, n % RING, k0:k1, :].rearrange("p k t -> p (k t)"),
                                             dbu, 0.0, ALU.mult, ALU.add).then_inc(scan, 1)
                    elif not last or it in ("gate", "resid0", "resid1"):
                        phase_a(nxt, it)

            for it in DVE_ORDER:
                if it[:2] not in ("pm", "sa", "bm", "sc"):
                    phase_a((0, 0), it)
            steps_of(dve, half_step)
            for it in ("gate", "resid0", "resid1"):
                phase_a((HS - 4, 5), it)

            newton2(1)
            dve.wait_ge(s_fw, 48)
            for c in range(B):
                for k in range(HK):
                    V.scalar_tensor_tensor(out=xc[:, k, c, :], in0=xs[c][:, k, :], scalar=fw[:, k:k + 1],
                                           in1=rstd2[:, c, :], op0=ALU.mult, op1=ALU.mult).then_inc(s_h1, 1)
            dve.wait_ge(s_h1, B * HK)
            V.tensor_tensor(h0[:, :, :, :].rearrange("p k b t -> p (k b t)"),
                            h0[:, :, :, :].rearrange("p k b t -> p (k b t)"),
                            xc[:, :, :, :].rearrange("p k b t -> p (k b t)"), ALU.add).then_inc(s_h1, 1)
            dve.wait_ge(s_h1, B * HK + 1)
            centre(1, h0)
            newton2(2)
            dve.wait_ge(s_xc, 4)
            for k in range(HK):
                V.tensor_tensor(xcf[:, k, :], xcf[:, k, :], rstd2[:, :, :].rearrange("p b t -> p (b t)"),
                                ALU.mult).then_inc(s_lno, 1)
            V.memset(gate[:, :, :], 0.0).then_inc(s_gate0, 1)
            V.tensor_copy(identb[:, :], ident[:, :]).then_inc(s_gate0, 1)
            dve.wait_ge(s_gatem, 1)
            dve.wait_ge(s_gate0, 2)
            V.tensor_copy(gate[:, 0:4, :], ps[:, 4, 0:4 * NE].rearrange("p (j e) -> p j e", j=4))
            V.tensor_copy(gate[0:2, 4:5, :], ps[0:2, 4, 4 * NE:5 * NE].rearrange("p (j e) -> p j e", j=1))\
                .then_inc(s_rt, 1)
            dve.wait_ge(s_rt, 1)
            V.tensor_reduce(mx[:, :], gate[:, :, :], AX.X, ALU.max).then_inc(s_route, 1)
            dve.wait_ge(s_route, 1)
            V.tensor_tensor(dif[:, :], mx[:, :], mx[:, :], ALU.subtract).then_inc(s_route, 1)
            V.tensor_tensor(eq[:, :, :], gate[:, :, :], mx[:, :].rearrange("p (j a) -> p j a", a=1)
                            .broadcast_to([128, 5, NE]), ALU.is_ge).then_inc(s_rt, 1)
            dve.wait_ge(s_rt, 2)
            dve.wait_ge(s_const, 5)
            io = iota8[:, :].rearrange("p (a e) -> p a e", a=1).broadcast_to([128, 5, NE])
            V.tensor_tensor(cand[:, :, :], eq[:, :, :], io, ALU.mult).then_inc(s_rt, 1)
            dve.wait_ge(s_rt, 3)
            V.tensor_reduce(first[:, :], cand[:, :, :], AX.X, ALU.min).then_inc(s_rt, 1)
            dve.wait_ge(s_rt, 4)
            V.tensor_tensor(oneh[:, :, :], io, first[:, :].rearrange("p (j a) -> p j a", a=1)
                            .broadcast_to([128, 5, NE]), ALU.is_equal).then_inc(s_rt, 1)
            dve.wait_ge(s_prob, 1)
            V.reciprocal(rden[:, :], prob[:, :]).then_inc(s_rt, 1)
            dve.wait_ge(s_rt, 6)
            V.tensor_tensor(pn[:, :], prob[:, :], rden[:, :], ALU.mult).then_inc(s_rt, 1)
            dve.wait_ge(s_rt, 7)
            V.tensor_tensor(disp[:, :, :], oneh[:, :, :], pn[:, :].rearrange("p (j a) -> p j a", a=1)
                            .broadcast_to([128, 5, NE]), ALU.mult).then_inc(s_disp, 1)

            dve.wait_ge(s_dispT, 1)
            V.tensor_copy(dispT[:, :], flat[0:NE, 2 * 512:2 * 512 + B * T]).then_inc(s_dispc, 1)
            for e in range(NE):
                dve.wait_ge(s_mask, e + 1)
                q = 2 * (e % 2)
                V.tensor_copy(maskb[:, e, :].rearrange("p (b t) -> p b t", b=B), ps[0:HP, q:q + 2, 0:T])\
                    .then_inc(s_maskc, 1)

            def expert(e, p):
                for j in range(B * FK):
                    n = FS[j // B]
                    dve.wait_ge(s_act, e * (B * FK) + (B * FK * p + j + 1))
                    if known_expert(e, p) or j >= HR:
                        dve.wait_ge(s_down, e * (B * FK) + (B * FK * p + j - HR + 1))
                    V.tensor_tensor(hf[0:n, j % HR, :], ps[0:n, 2 * (j % 2) + 1, 0:T], sg[0:n, j % 2, :], ALU.mult)\
                        .then_inc(s_fmul, 1)

            experts_of(dve, expert)

        @block.tensor
        def _(pe):
            M = pe.matmul
            pe.wait_ge(s_gather12, 16 * 10)
            pe.wait_ge(s_const, 1)
            for k in range(2):
                for b in range(B):
                    pe.transpose(ps[0:48, 5, b * 256 + k * 128:b * 256 + (k + 1) * 128],
                                 G2[:, k, 48 * b:48 * b + 48], ident[:, :])
            for q in range(8):
                for b in range(B):
                    c0 = (1 + 2 * b) * 512 + q * 128
                    ins = pe.transpose(flat[0:12, c0:c0 + 128], G1[:, q, 12 * b:12 * b + 12], ident[:, :])
            ins.then_inc(s_gt, 1)
            pe.wait_ge(s_gtc, 3)
            pe.wait_ge(s_tokw, 160)
            pe.wait_ge(s_cself, 1)
            for lvl, n, gt_, w_, br, c0 in ((1, 64, GT1, w1, b1r, 0), (2, 16, GT2, w2, b2r, 128)):
                for b in range(B):
                    o = ps[0:n, 7, c0 + b * EMB:c0 + (b + 1) * EMB]
                    for g in range(GP):
                        M(o, gt_[:, b * n * GP + g:(b + 1) * n * GP:GP], w_[:, g, :], start=(g == 0), stop=False)
                    ins = M(o, ones[0:1, 0:n], br[:, :], start=False, stop=True)
            ins.then_inc(s_tokm, 1)
            pe.wait_ge(s_tokc, 2)
            for b in range(B):
                M(ps[0:EMB, 0, b * 256:(b + 1) * 256], tok1[:, b, :], m1[:, :], start=True, stop=True)
                ins = M(ps[0:EMB, 1, b * 256:(b + 1) * 256], tok2[:, b, :], m2[:, :], start=True, stop=True)
            ins.then_inc(s_int, 1)

            def fuse(k, lvl, start, stop):
                return M(ps[0:HP, 2 + k, :], wf[:, lvl, k * HP:(k + 1) * HP], cat[:, lvl, :], start=start, stop=stop)

            pe.wait_ge(s_intc, 1)
            for k in range(HK):
                fuse(k, 1, True, False)
                fuse(k, 2, False, False)
            pe.wait_ge(s_g0b, B)
            for k in range(2):
                for b in range(B):
                    ins = pe.transpose(ps[0:48, 4, b * 256 + k * 128:b * 256 + (k + 1) * 128], G0b[:, k, b, :],
                                       ident[:, :])
            ins.then_inc(s_gt, 1)
            pe.wait_ge(s_gtc, 4)
            M(ps[0:EMB, 6, :], w0[:, :], GT0[:, :], start=True, stop=True).then_inc(s_tokm, 1)
            pe.wait_ge(s_tokc, 3)
            for k in range(HK):
                ins = fuse(k, 0, False, True)
            ins.then_inc(s_fuse, 1)

            def over_features(bank, src, b):
                for k in range(HK):
                    ins = M(ps[0:HP, bank, 0:T], ones[0:HP, 0:HP], src[:, k, b, :], start=(k == 0), stop=(k == HK - 1))
                return ins

            def squares(r):
                pe.wait_ge(s_sq2, r + 1)
                for b in range(B):
                    ins = over_features(2 + b, sq2, b)
                ins.then_inc(s_ss2, 1)

            pe.wait_ge(s_h0, 4)
            for b in range(B):
                over_features(b, h0, b).then_inc(s_sum, 1)
            squares(0)

            def spread_b(st, n):
                c = st[1] % 2
                if n >= 2 or known(st, 1):
                    pe.wait_ge(s_bmul, cnt(N, st, 0, n - 1))
                if n == 0:
                    pe.wait_ge(s_lo, cnt(1, st, 1))
                M(ps[:, BB + n % 2, 0:T], sel[:, n, :], bcs[c][:, :], start=True, stop=True).then_inc(s_bb, 1)

            def phase_a(st, it):
                off = st[1]
                c = off % 2
                p = (off // 2) % 2
                po = ((off - 2) // 2) % 2
                if it[:4] == "outp" and known(st, 2):
                    k = int(it[4:])
                    if k == 0:
                        pe.wait_ge(s_gate, cnt(1, st, -1))
                        pe.wait_ge(s_ow[po], cnt4(16, st, off - 2))
                        if isinstance(st[0], int):
                            pe.wait_ge(s_cc, N * min(st[0] + off, HS))
                        else:
                            pe.wait_ge(s_cc, cnt(N, st, 0))
                    for j in range(IK):
                        ins = M(ps[0:HP, BA + k, 0:T], outw[po][:, j, k * HP:(k + 1) * HP], gt[:, j, :],
                                start=(j == 0), stop=(j == IK - 1))
                    ins.then_inc(s_outp, 1)
                if it[:2] == "ss":
                    k = int(it[2:])
                    pe.wait_ge(s_sq, cnt(HK, st, 0, k + 1))
                    if k == 0 and known(st, 1):
                        pe.wait_ge(s_cc, cnt(N, st, 0))
                    ins = M(ps[0:HP, BA, 0:T], ones[0:HP, 0:HP], sq[:, k, :], start=(k == 0), stop=(k == HK - 1))
                    if k == HK - 1:
                        ins.then_inc(s_ss, 1)
                if it[:3] == "inp":
                    m = int(it[3:])
                    if m == 0:
                        pe.wait_ge(s_xn, cnt(1, st, 1))
                        pe.wait_ge(s_w[p], cnt4(16 * NW, st, off))
                    if m >= 2:
                        pe.wait_ge(s_evac, cnt(2 * IK, st, 0, m - 1))
                    for k in range(HK):
                        ins = M(ps[:, BA + (m + 1) % 2, 0:T], inw[p][:, k, m * 128:(m + 1) * 128], xn[:, k, :],
                                start=(k == 0), stop=(k == HK - 1))
                    ins.then_inc(s_inp, 1)
                if it == "xproj":
                    pe.wait_ge(s_silu, cnt(2, st, 0, 1))
                    if off < 2 and known(st, 0):
                        pe.wait_ge(s_cself, 6)
                    for k in range(IK):
                        ins = M(ps[0:96, BA + 1, 0:T], xpw[p][:, k, :], uz[c][:, k, :],
                                start=(k == 0), stop=(k == IK - 1))
                    ins.then_inc(s_xproj, 1)
                if it[:3] == "dtp":
                    m = int(it[3:])
                    if m == 0:
                        pe.wait_ge(s_dtr, cnt(1, st, 1))
                    if m == 1:
                        pe.wait_ge(s_r1, cnt(1, st, 1))
                    if m == 2:
                        pe.wait_ge(s_xpre, cnt(IK, st, 0, 1))
                    M(ps[:, BA + m % 2, 0:T], dtw[p][:, m * 128:(m + 1) * 128], dtr[:, :],
                      start=True, stop=True).then_inc(s_dtp, 1)
                if it[:2] == "cb":
                    n = int(it[2:])
                    if n == 0:
                        pe.wait_ge(s_lo, cnt(1, st, 1))
                        pe.wait_ge(s_xpre, cnt(IK, st, 1))
                    if n >= 2:
                        pe.wait_ge(s_cc, cnt(N, st, 0, n - 1))
                    M(ps[:, BA + n % 2, 0:T], sel[:, N + n, :], bcs[c][:, :], start=True, stop=True)\
                        .then_inc(s_cb, 1)

            def sum_states(st, n):
                c, p = st[1] % 2, (st[1] // 2) % 2
                parts = ((BY, 0, 512), (BY + 1, 512, W3T))
                if n == 0:
                    if known(st, 1):
                        pe.wait_ge(s_gate, cnt(1, st, 0))
                    pe.wait_ge(s_diag, cnt(1, st, 1 + (st[1] + 1) % 2))
                    for bank, a, z in parts:
                        for k in range(IK):
                            lo, hi = max(a, k * T), min(z, (k + 1) * T)
                            if lo < hi:
                                M(ps[:, bank, lo - a:hi - a], diagD[p][:, k, :], uz[c][:, k, lo - k * T:hi - k * T],
                                  start=(lo == a), stop=False)
                pe.wait_ge(s_cmul, cnt(N, st, 0, n + 1))
                for bank, a, z in parts:
                    ins = M(ps[:, bank, 0:z - a], ident[:, :], hc[:, n % RING, a:z], start=False, stop=(n == N - 1))
                ins.then_inc(s_ys, 1)

            def half_step(st, off):
                nxt, last = (st[0], off + 1), is_last(st)
                for it in PE_ORDER:
                    if it[:2] == "bb":
                        spread_b(st, int(it[2:]))
                    elif it[:2] == "ys":
                        sum_states(st, int(it[2:]))
                    elif it[:4] == "next":
                        if not last:
                            spread_b(nxt, int(it[4:]))
                    elif not last or it[:4] == "outp":
                        phase_a(nxt, it)

            pe.wait_ge(s_const, 4)
            for it in PE_ORDER:
                if it[:2] not in ("bb", "ys") and it[:4] != "next":
                    phase_a((0, 0), it)
            for n in range(2):
                spread_b((0, 0), n)
            steps_of(pe, half_step)
            for k in range(HK):
                phase_a((HS - 4, 5), f"outp{k}")

            squares(1)
            pe.wait_ge(s_h1, B * HK + 1)
            for b in range(B):
                over_features(b, h0, b).then_inc(s_sum, 1)
            squares(2)
            pe.wait_ge(s_lno, 4)
            pe.wait_ge(s_fw, 48)
            for j in range(5):
                n = min(128, B * T - 128 * j)
                o = ps[0:n, 4, j * NE:(j + 1) * NE]
                for k in range(HK):
                    M(o, xcf[:, k, 128 * j:128 * j + n], wg[:, k, :], start=(k == 0), stop=False)
                ins = M(o, ones[0:1, 0:n], bgr[:, :], start=False, stop=True)
            ins.then_inc(s_gatem, 1)
            pe.wait_ge(s_disp, 1)
            for j in range(5):
                n = min(128, B * T - 128 * j)
                ins = M(flat[0:NE, 2 * 512 + 128 * j:2 * 512 + 128 * j + n], disp[0:n, j, :], identb[0:n, 0:n],
                        start=True, stop=True)
            ins.then_inc(s_dispT, 1)
            pe.wait_ge(s_dispc, 1)
            for e in range(NE):
                if e >= 2:
                    pe.wait_ge(s_maskc, e - 1)
                for b in range(B):
                    ins = M(ps[0:HP, 2 * (e % 2) + b, 0:T], sel[0:NE, e, 0:HP], dispT[:, b * T:(b + 1) * T],
                            start=True, stop=True)
                ins.then_inc(s_mask, 1)

            def down(e, p, j):
                n = FS[j // B]
                pe.wait_ge(s_fmul, e * (B * FK) + (B * FK * p + j + 1))
                for k in range(HK):
                    ins = M(ps[0:HP, 4 + 2 * k + j % B, 0:T], e3[p][0:n, j // B, k * HP:(k + 1) * HP],
                            hf[0:n, j % HR, :],
                            start=(j < B and not known_expert(e, p)), stop=False)
                ins.then_inc(s_down, 1)

            def expert(e, p):
                pe.wait_ge(s_e[p], e * 32 + 64)
                pe.wait_ge(s_xmask, e + (p + 1))
                if not known_expert(e, p):
                    pe.wait_ge(s_maskc, NE)
                for j in range(B * FK):
                    ft, b = divmod(j, B)
                    n = FS[ft]
                    if known_expert(e, p) or j >= 2:
                        pe.wait_ge(s_fmul, e * (B * FK) + (B * FK * p + j - 1))
                    q = 2 * (j % 2)
                    for k in range(HK):
                        M(ps[0:n, q, 0:T], e1[p][:, k, 128 * ft:128 * ft + n], xcf[:, k, b * T:(b + 1) * T],
                          start=(k == 0), stop=(k == HK - 1))
                    for k in range(HK):
                        ins = M(ps[0:n, q + 1, 0:T], e2[p][:, k, 128 * ft:128 * ft + n],
                                xm[p][:, k, b * T:(b + 1) * T], start=(k == 0), stop=(k == HK - 1))
                    ins.then_inc(s_up, 1)
                    if j >= 1:
                        down(e, p, j - 1)
                down(e, p, B * FK - 1)

            experts_of(pe, expert)
            for k in range(HK):
                for b in range(B):
                    ins = M(ps[0:HP, 4 + 2 * k + b, 0:T], ident[0:HP, 0:HP], h0[:, k, b, :], start=False, stop=True)
            ins.then_inc(s_resid2, 1)
            pe.wait_ge(s_outT, HK)
            for b in range(B):
                for k, (t0, n) in enumerate(((0, 128), (128, 128), (256, 1))):
                    j = 3 * b + k
                    if j >= 4:
                        pe.wait_ge(s_outs, j - 3)
                    for q in range(HK):
                        ins = pe.transpose(ps[0:n, j % 4, q * HP:(q + 1) * HP], outT[:, q, b, t0:t0 + n],
                                           ident[0:HP, 0:HP])
                    ins.then_inc(s_tr, 1)


def kernel(**inputs):
    import numpy as _np
    import concourse.bacc as _bacc
    from concourse import mybir as _mybir
    from concourse.bass_utils import run_bass_kernel_spmd as _run

    v = {n: _np.asarray(a) for n, a in inputs.items()}
    x = v["x"]

    def patches(p):
        h = x.shape[2] // p
        return x.reshape(2, 3, h, p, h, p).transpose(2, 4, 0, 3, 5, 1).reshape(h * h, -1)

    def by_patch(w, p):
        return w.reshape(EMB, GP, 3 * p * p).transpose(2, 1, 0)

    def halves(w):
        return _np.moveaxis(w.reshape(*w.shape[:-1], HK, HP), -1, -2)

    def interpolation(length):
        m = _np.zeros((length, 256), _np.float32)
        pos = _np.clip((_np.arange(256) + 0.5) * (length / 256) - 0.5, 0, length - 1)
        lo = _np.floor(pos).astype(int)
        for t in range(256):
            m[lo[t], t] += 1 - (pos[t] - lo[t])
            m[min(lo[t] + 1, length - 1), t] += pos[t] - lo[t]
        return m

    a, t = "L0_attn_", "L0_tok_"
    prm = _np.concatenate([v[a + "conv_w"][:, :, 0, :]] + [v[a + n][:, :, None] for n in ("conv_b", "dt_proj_b", "D")]
                          + [v[a + "A_log"]], axis=2)
    lay = dict(
        P0=patches(1), P1=patches(2), P2=patches(4), idx0=v[t + "idx0"].reshape(2, 128, GP).transpose(1, 0, 2),
        idx1=v[t + "idx1"].reshape(8, 128).T, idx2=v[t + "idx2"].reshape(2, 128).T,
        W0T=v[t + "W0"].T, W1G=by_patch(v[t + "W1"], 2), W2G=by_patch(v[t + "W2"], 4),
        b0=v[t + "b0"][:, None], b1=v[t + "b1"], b2=v[t + "b2"], WfT=v[t + "Wf"].T, bf=halves(v[t + "bf"]),
        M1=interpolation(64), M2=interpolation(16), cls=halves(v["cls_tok"][0, 0]),
        in_wT=v[a + "in_proj_w"].transpose(0, 2, 1), x_wT=v[a + "x_proj_w"].transpose(0, 2, 1),
        dt_wT=v[a + "dt_proj_w"].transpose(0, 2, 1), out_wT=v[a + "out_proj_w"].transpose(0, 2, 1),
        prm_d=prm, norm_w=halves(v[a + "norm_w"]), final_w=halves(v[a + "final_norm_w"]),
        WgT=v["L0_ffn_Wg"].T, bg=v["L0_ffn_bg"], E1=v["L0_ffn_W1"].transpose(0, 2, 1),
        E2=v["L0_ffn_W2"].transpose(0, 2, 1), E3=v["L0_ffn_W3"].transpose(0, 2, 1))
    nc = _bacc.Bacc("TRN2", target_bir_lowering=False, num_devices=1)
    arrays, args = {}, {}
    for name, arr in lay.items():
        arr = _np.ascontiguousarray(arr)
        arrays[f"in_{name}"] = arr
        args[name] = nc.dram_tensor(f"in_{name}", arr.shape, _mybir.dt.from_np(arr.dtype), kind="ExternalInput").ap()
    out = nc.dram_tensor("out_h", (B, T, H), F32, kind="ExternalOutput").ap()
    mamba_vit(nc, out=out, **args)
    return _run(nc, [arrays], core_ids=[0]).results[0]["out_h"]
```
